# Optimizing a Trainium2 kernel written in Bass

```python
import numpy as np
import jax
import jax.numpy as jnp

def _softmax(x, axis=-1):
    return jax.nn.softmax(x, axis=axis)

def _gelu(x):
    return jax.nn.gelu(x, approximate=True)

def _silu(x):
    return jax.nn.silu(x)

def _sigmoid(x):
    return jax.nn.sigmoid(x)

def _layernorm(x, axis=-1, eps=1e-05):
    m = jnp.mean(x, axis=axis, keepdims=True)
    v = jnp.var(x, axis=axis, keepdims=True)
    return (x - m) / jnp.sqrt(v + eps)

def _scatter_add(tgt, idx, src, axis=0):
    return tgt.at[idx].add(src)

def _segment_sum(src, seg, n):
    return jax.ops.segment_sum(src, seg, n)
kernel_name = 'mk_gps_d1_gnn_r8_133619'

def setup_inputs(seed: int=0):
    np.random.seed(seed)
    _w = jnp.asarray

    def _rec_inputs():
        import jax
        import jax.numpy as jnp
        _gk = jax.random.key(seed)
        x = -0.0002117 + 1 * jax.random.normal(jax.random.fold_in(_gk, 1), (12500, 256), jnp.float32)
        _s = jax.random.randint(jax.random.fold_in(_gk, 2), (100000,), 0, 12500, jnp.int32)
        _d = jax.random.randint(jax.random.fold_in(_gk, 3), (100000,), 0, 12500, jnp.int32)
        _loop = jnp.arange(12500, dtype=jnp.int32)
        src = jnp.concatenate([_s, _d, _loop])
        dst = jnp.concatenate([_d, _s, _loop])
        _o = jnp.argsort(dst, stable=True)
        src = src[_o]
        dst = dst[_o]
        edge_weight = jax.random.uniform(jax.random.fold_in(_gk, 12), (212500,), jnp.float32, 0.0, 0.03125)
        return (x, src, dst, edge_weight)
    x, src, dst, edge_weight = _rec_inputs()

    def _L0_gnn_setup():
        import jax, jax.numpy as jnp
        import numpy as np
        N_NODES = 12500
        N_EDGES = 400000
        DIM = 256
        LEAKY_SLOPE = 0.2
        EPS = 1e-12
        key = jax.random.key(seed)
        ks = jax.random.split(key, 8)
        embeddings = jax.random.normal(ks[0], (N_NODES, DIM), dtype=jnp.float32)
        edge_src = jax.random.randint(ks[1], (N_EDGES,), 0, N_NODES, dtype=jnp.int32)
        edge_dst = jax.random.randint(ks[2], (N_EDGES,), 0, N_NODES, dtype=jnp.int32)
        edge_val = jax.random.uniform(ks[3], (N_EDGES,), dtype=jnp.float32) / 32.0
        scale = 1.0 / np.sqrt(DIM)
        W1 = jax.random.normal(ks[4], (DIM, DIM), dtype=jnp.float32) * scale
        b1 = jax.random.normal(ks[5], (DIM,), dtype=jnp.float32) * 0.01
        W2 = jax.random.normal(ks[6], (DIM, DIM), dtype=jnp.float32) * scale
        b2 = jax.random.normal(ks[7], (DIM,), dtype=jnp.float32) * 0.01
        return {'embeddings': embeddings, 'edge_src': edge_src, 'edge_dst': edge_dst, 'edge_val': edge_val, 'W1': W1, 'b1': b1, 'W2': W2, 'b2': b2}
    _L0_gnn_all = _L0_gnn_setup()
    _L0_gnn_in = {k: v for k, v in _L0_gnn_all.items() if k in ('W1', 'b1', 'W2', 'b2')}
    del _L0_gnn_all

    def _L0_mix_setup():
        import jax, jax.numpy as jnp
        import numpy as np
        MIDC = 256
        HEADS = 8
        HEADC = MIDC // HEADS
        EPS = 1e-05

        def _ln(x, gamma, beta):
            mu = jnp.mean(x, axis=-1, keepdims=True)
            var = jnp.var(x, axis=-1, keepdims=True)
            return (x - mu) * jax.lax.rsqrt(var + EPS) * gamma + beta
        key = jax.random.key(seed)
        ks = jax.random.split(key, 8)
        B, HW, C = (8, 512, MIDC)
        s = 1.0 / np.sqrt(C)
        return {'x': jax.random.normal(ks[0], (B, HW, C), jnp.float32), 'w_qkv': jax.random.normal(ks[1], (C, 3 * C), jnp.float32) * s, 'b_qkv': jnp.zeros((3 * C,), jnp.float32), 'kln_g': jnp.ones((HEADC,), jnp.float32), 'kln_b': jnp.zeros((HEADC,), jnp.float32), 'vln_g': jnp.ones((HEADC,), jnp.float32), 'vln_b': jnp.zeros((HEADC,), jnp.float32), 'w1': jax.random.normal(ks[2], (C, C), jnp.float32) * s, 'b1': jnp.zeros((C,), jnp.float32), 'w2': jax.random.normal(ks[3], (C, C), jnp.float32) * s, 'b2': jnp.zeros((C,), jnp.float32)}
    _L0_mix_all = _L0_mix_setup()
    _L0_mix_in = {k: v for k, v in _L0_mix_all.items() if k in ('w_qkv', 'b_qkv', 'kln_g', 'kln_b', 'vln_g', 'vln_b', 'w1', 'b1', 'w2', 'b2')}
    del _L0_mix_all

    def _L0_ffn_setup():
        import math
        import jax, jax.numpy as jnp
        import numpy as np
        CAPACITY_FACTOR = 1.25
        key = jax.random.key(seed)
        ks = jax.random.split(key, 5)
        B, L, D, F, E = (8, 1024, 256, 1024, 8)
        h = jax.random.normal(ks[0], (B, L, D), dtype=jnp.float32)
        gate_w = jax.random.normal(ks[1], (D, E), dtype=jnp.float32) * 0.02
        gate_b = jnp.zeros((E,), dtype=jnp.float32)
        w1 = jax.random.normal(ks[2], (E, D, F), dtype=jnp.float32) * (1.0 / math.sqrt(D))
        b1 = jnp.zeros((E, F), dtype=jnp.float32)
        w2 = jax.random.normal(ks[3], (E, F, D), dtype=jnp.float32) * (1.0 / math.sqrt(F))
        b2 = jnp.zeros((E, D), dtype=jnp.float32)
        return {'h': h, 'gate_w': gate_w, 'gate_b': gate_b, 'w1': w1, 'b1': b1, 'w2': w2, 'b2': b2}
    _L0_ffn_all = _L0_ffn_setup()
    _L0_ffn_in = {k: v for k, v in _L0_ffn_all.items() if k in ('gate_w', 'gate_b', 'w1', 'b1', 'w2', 'b2')}
    del _L0_ffn_all
    return {'x': x, 'src': src, 'dst': dst, 'edge_weight': edge_weight, 'L0_gnn_W1': _L0_gnn_in['W1'], 'L0_gnn_b1': _L0_gnn_in['b1'], 'L0_gnn_W2': _L0_gnn_in['W2'], 'L0_gnn_b2': _L0_gnn_in['b2'], 'L0_mix_w_qkv': _L0_mix_in['w_qkv'], 'L0_mix_b_qkv': _L0_mix_in['b_qkv'], 'L0_mix_kln_g': _L0_mix_in['kln_g'], 'L0_mix_kln_b': _L0_mix_in['kln_b'], 'L0_mix_vln_g': _L0_mix_in['vln_g'], 'L0_mix_vln_b': _L0_mix_in['vln_b'], 'L0_mix_w1': _L0_mix_in['w1'], 'L0_mix_b1': _L0_mix_in['b1'], 'L0_mix_w2': _L0_mix_in['w2'], 'L0_mix_b2': _L0_mix_in['b2'], 'L0_ffn_gate_w': _L0_ffn_in['gate_w'], 'L0_ffn_gate_b': _L0_ffn_in['gate_b'], 'L0_ffn_w1': _L0_ffn_in['w1'], 'L0_ffn_b1': _L0_ffn_in['b1'], 'L0_ffn_w2': _L0_ffn_in['w2'], 'L0_ffn_b2': _L0_ffn_in['b2']}

def reference(x, src, dst, edge_weight, L0_gnn_W1, L0_gnn_b1, L0_gnn_W2, L0_gnn_b2, L0_mix_w_qkv, L0_mix_b_qkv, L0_mix_kln_g, L0_mix_kln_b, L0_mix_vln_g, L0_mix_vln_b, L0_mix_w1, L0_mix_b1, L0_mix_w2, L0_mix_b2, L0_ffn_gate_w, L0_ffn_gate_b, L0_ffn_w1, L0_ffn_b1, L0_ffn_w2, L0_ffn_b2):
    import jax
    import jax.numpy as jnp

    def _L0_gnn_ref(embeddings, edge_src, edge_dst, edge_val, W1, b1, W2, b2):
        import jax, jax.numpy as jnp
        import numpy as np
        N_NODES = 12500
        N_EDGES = 400000
        DIM = 256
        LEAKY_SLOPE = 0.2
        EPS = 1e-12
        ego_emb = embeddings @ W1.T + b1
        messages = edge_val[:, None] * embeddings[edge_src]
        neighbor_emb = jax.ops.segment_sum(messages, edge_dst, num_segments=embeddings.shape[0])
        interaction_emb = neighbor_emb * embeddings
        side_emb = (neighbor_emb + interaction_emb) @ W2.T + b2
        out = ego_emb + side_emb
        out = jnp.where(out >= 0, out, LEAKY_SLOPE * out)
        norm = jnp.sqrt(jnp.sum(out * out, axis=1, keepdims=True))
        return out / jnp.maximum(norm, EPS)

    def _L0_mix_ref(x, w_qkv, b_qkv, kln_g, kln_b, vln_g, vln_b, w1, b1, w2, b2):
        import jax, jax.numpy as jnp
        import numpy as np
        MIDC = 256
        HEADS = 8
        HEADC = MIDC // HEADS
        EPS = 1e-05

        def _ln(x, gamma, beta):
            mu = jnp.mean(x, axis=-1, keepdims=True)
            var = jnp.var(x, axis=-1, keepdims=True)
            return (x - mu) * jax.lax.rsqrt(var + EPS) * gamma + beta
        B, HW, C = x.shape
        bias = x
        qkv = (x @ w_qkv + b_qkv).reshape(B, HW, HEADS, 3 * HEADC)
        qkv = qkv.transpose(0, 2, 1, 3)
        q, k, v = jnp.split(qkv, 3, axis=-1)
        k = _ln(k, kln_g, kln_b)
        v = _ln(v, vln_g, vln_b)
        kv = jnp.einsum('bhnd,bhne->bhde', k, v) / HW
        out = jnp.einsum('bhnd,bhde->bhne', q, kv)
        out = out.transpose(0, 2, 1, 3).reshape(B, HW, C)
        ret = out + bias
        h = jax.nn.gelu(ret @ w1 + b1, approximate=False)
        return h @ w2 + b2 + bias

    def _L0_ffn_ref(h, gate_w, gate_b, w1, b1, w2, b2):
        import math
        import jax, jax.numpy as jnp
        import numpy as np
        CAPACITY_FACTOR = 1.25
        B, L, D = h.shape
        E = gate_w.shape[1]
        T = B * L
        C = max(1, math.ceil(CAPACITY_FACTOR * T / E))
        x = h.reshape(T, D)
        logits = x @ gate_w + gate_b
        probs = jax.nn.softmax(logits, axis=-1)
        idx = jnp.argmax(probs, axis=-1)
        prb = jnp.take_along_axis(probs, idx[:, None], axis=1)[:, 0]
        one_hot = jax.nn.one_hot(idx, E, dtype=jnp.float32)
        pos = (jnp.cumsum(one_hot, axis=0) * one_hot).sum(-1).astype(jnp.int32) - 1
        kept = pos < C
        pos_safe = jnp.where(kept, pos, C)
        buf = jnp.zeros((E, C, D), dtype=h.dtype).at[idx, pos_safe].set(x, mode='drop')
        hmid = jax.nn.relu(jnp.einsum('ecd,edf->ecf', buf, w1) + b1[:, None, :])
        ybuf = jnp.einsum('ecf,efd->ecd', hmid, w2) + b2[:, None, :]
        pos_g = jnp.minimum(pos, C - 1)
        y_tok = ybuf[idx, pos_g] * (prb * kept)[:, None]
        y = y_tok.reshape(B, L, D)
        y = jnp.nan_to_num(y, nan=0.0, posinf=10000.0, neginf=-10000.0)
        return y
    xn = _layernorm(x, axis=-1)
    x = x + _L0_gnn_ref(xn, src, dst, edge_weight, L0_gnn_W1, L0_gnn_b1, L0_gnn_W2, L0_gnn_b2) + _L0_mix_ref(xn[None], L0_mix_w_qkv, L0_mix_b_qkv, L0_mix_kln_g, L0_mix_kln_b, L0_mix_vln_g, L0_mix_vln_b, L0_mix_w1, L0_mix_b1, L0_mix_w2, L0_mix_b2)[0]
    x = x + _L0_ffn_ref(_layernorm(x, axis=-1)[None], L0_ffn_gate_w, L0_ffn_gate_b, L0_ffn_w1, L0_ffn_b1, L0_ffn_w2, L0_ffn_b2)[0]
    return x

_drawn_inputs = setup_inputs


def setup_inputs(seed=0):
    import zlib

    import numpy as np

    out = dict(_drawn_inputs(seed))
    spreads = {'L0_mix_b_qkv': (0.0, 0.1),
     'L0_mix_kln_g': (1.0, 0.6),
     'L0_mix_kln_b': (0.0, 0.39),
     'L0_mix_vln_g': (1.0, 0.547),
     'L0_mix_vln_b': (0.0, 0.36),
     'L0_mix_b1': (0.0, 0.1),
     'L0_mix_b2': (0.0, 0.1),
     'L0_ffn_gate_b': (0.0, 0.1),
     'L0_ffn_b1': (0.0, 0.8),
     'L0_ffn_b2': (0.0, 0.8)}
    factors = {'edge_weight': 8.0, 'L0_gnn_b1': 8.0, 'L0_gnn_W2': 8.0, 'L0_gnn_b2': 8.0}
    for name, (base, spread) in spreads.items():
        noise = np.random.default_rng([zlib.crc32(name.encode()), seed]).standard_normal(out[name].shape)
        drawn = base * np.exp(spread * noise) if base else spread * noise
        out[name] = jnp.asarray(drawn.astype(out[name].dtype))
    for name, factor in factors.items():
        out[name] = (out[name] * factor).astype(out[name].dtype)
    return out
```

```python
import math
from contextlib import ExitStack

import concourse.bass as bass
from concourse import mybir

F32 = mybir.dt.float32
I32 = mybir.dt.int32
ALU = mybir.AluOpType
ACT = mybir.ActivationFunctionType
AX = mybir.AxisListType

P = 128
GROUP = 4
WIN = 48
WIDE = 500
EPS = 1e-5
NORM_EPS = 1e-12
LEAKY = 0.2
HEADC = 32
CAPACITY_FACTOR = 1.25


class Lane:

    def __init__(self, done):
        self.done, self.count, self.steps, self.waited = done, 0, [], {}

    def wait(self, *marks):
        for sem, value in marks:
            if self.waited.get(sem, 0) < value:
                self.waited[sem] = value
                self.steps.append(lambda e, s=sem, v=value: e.wait_ge(s, v))

    def run(self, step, tell=True):
        if not tell:
            self.steps.append(step)
            return None
        self.count += 1
        self.steps.append(lambda e: step(e).then_inc(self.done, 1))
        return self.done, self.count

    def chain(self, step):
        mark = self.run(step)
        self.wait(mark)
        return mark

    def dma(self, step, slot):
        slot[1] += 16
        self.steps.append(lambda e, s=slot[0]: step(e).then_inc(s, 16))
        return slot[0], slot[1]

    def play(self, engine):
        for step in self.steps:
            step(engine)


def run_skewed(pipeline, ticks):
    live = []
    for unit in pipeline:
        live.append(unit)
        live = [u for u in live if next(u, "end") != "end"]
        yield
    while live:
        live = [u for u in live if next(u, "end") != "end"]
        yield


def build(nc, x, src, dst, weight, dst_grouped, gnn_w1t, gnn_b1, gnn_w2t, gnn_b2,
          wqt_bq, wkv, bkv, kv_gamma, kv_beta, mix_w1, mix_b1, mix_w2, mix_b2,
          gate_w, gate_b, ffn_w1, ffn_b1, ffn_w2, ffn_b2, out):
    N, D = x.shape
    H = D // P
    T = -(-N // P)
    GROUPS = src.shape[1] // GROUP
    CHUNKS = src.shape[1]
    NE = gate_w.shape[1]
    FF = ffn_w1.shape[2]
    FC = FF // P
    CAP = max(1, math.ceil(CAPACITY_FACTOR * N / NE))
    SLOT_TILES = -(-CAP // P)
    TABLE = NE * SLOT_TILES
    WIDE_WINDOWS = -(-N // WIDE)
    ACC_W = max(WIDE_WINDOWS * WIDE, T * P, N + WIN)
    GE = 4
    EXPERT_W = H * FF + FC * D + D
    ROUTE_AT = 2 * EXPERT_W + 2 * FC * GE * P
    RT = 4
    ROUTE_W = 4 * T * NE + 7 * T + (3 * RT + 2) * P
    ACC_W = max(ACC_W, -(-(ROUTE_AT + ROUTE_W) // H))
    HEADS = D // HEADC
    GP, GJ = dst_grouped.shape[0], dst_grouped.shape[1] // (GROUP * P)
    assert GP * GJ == GROUPS and TABLE <= P and D == 2 * P

    def rows(t):
        return min(P, N - t * P)

    ctx = ExitStack()
    with ctx:
        def sb(name, shape, dt=F32):
            return ctx.enter_context(nc.sbuf_tensor(name, shape, dt))

        def sem(name):
            return ctx.enter_context(nc.semaphore(name))

        def slot(name):
            return [sem(name), 0]

        xn_d = nc.dram_tensor("xn_scratch", [N, D], F32).ap()
        xnt_d = nc.dram_tensor("xnt_scratch", [H, P, T * P], F32).ap()
        base_d = nc.dram_tensor("base_scratch", [N, D], F32).ap()
        ego_d = nc.dram_tensor("ego_scratch", [N, D], F32).ap()
        comb_d = nc.dram_tensor("comb_scratch", [N, 2 * D], F32).ap()
        gmin_d = nc.dram_tensor("group_min_scratch", [GROUPS], I32).ap()

        acc = sb("acc", [P, H, ACC_W])
        src_sb = sb("src_sb", [P, CHUNKS], I32)
        rel_sb = sb("rel_sb", [P, CHUNKS])
        wgt_sb = sb("wgt_sb", [P, CHUNKS])
        gmin_sb = sb("gmin_sb", [P, GROUPS], I32)
        iota_win = sb("iota_win", [P, WIN])
        iota_p = sb("iota_p", [P, P])
        ident = sb("ident", [P, P])
        upper = sb("upper", [P, P])
        ones = sb("ones", [P, P])
        eps_sb = sb("eps_sb", [P, 1])
        ROW_SLOTS = 4 * GROUP
        rows_sb = sb("rows_sb", [P, ROW_SLOTS, D])
        S_SLOTS, S_GROUPS = 3, 2
        s_sb = sb("s_sb", [P, S_SLOTS, S_GROUPS * GROUP, WIN])
        ARENA = 12 * 1024
        arena = sb("arena", [P, ARENA])

        psum = [ctx.enter_context(nc.psum_tensor(f"bank{i}", [P, 512], F32)) for i in range(8)]

        sp, pool, pe, dve, act = (Lane(sem(f"done_{n}")) for n in ("sp", "pool", "pe", "dve", "act"))

        taken = [0]

        def carve(shape, reset=None):
            if reset is not None:
                taken[0] = reset
            n = math.prod(shape)
            at = taken[0]
            taken[0] += n
            assert taken[0] <= ARENA, (taken[0], ARENA)
            v = arena[:, at:at + n]
            if len(shape) == 2:
                v = v.rearrange("p (a b) -> p a b", a=shape[0])
            elif len(shape) == 3:
                v = v.rearrange("p (a b c) -> p a b c", a=shape[0], b=shape[1])
            return v

        ld_gmin, ld_edges, ld_gbc = slot("ld_gmin"), slot("ld_edges"), slot("ld_gbc")
        grouped = acc[0:GP, 0, 0:GJ * GROUP * P].bitcast(I32)
        got_grouped = sp.dma(lambda e: e.dma_start(grouped, dst_grouped), ld_gmin)
        for to, frm in ((src_sb[:, :], src), (rel_sb[:, :].bitcast(I32), dst), (wgt_sb[:, :], weight)):
            got_edges = sp.dma(lambda e, to=to, frm=frm: e.dma_start(to, frm), ld_edges)

        pool.run(lambda e: e.iota(iota_win[:, :], [[1, WIN]], base=0, channel_multiplier=0,
                                  allow_small_or_imprecise_dtypes=True))
        pool.run(lambda e: e.iota(iota_p[:, :], [[1, P]], base=0, channel_multiplier=0,
                                  allow_small_or_imprecise_dtypes=True))
        pool.run(lambda e: e.memset(ident[:, :], 0.0))
        pool.run(lambda e: e.memset(eps_sb[:, :], EPS))
        pool.chain(lambda e: e.memset(ones[:, :], 1.0))
        pool.run(lambda e: e.affine_select(out=ident[:, :], in_=ident[:, :], compare_op=ALU.not_equal,
                                           fill=1.0, base=0, pattern=[[-1, P]], channel_multiplier=1))
        consts_ready = pool.run(lambda e: e.affine_select(
            out=upper[:, :], in_=ones[:, :], compare_op=ALU.is_ge, fill=0.0, base=0,
            pattern=[[1, P]], channel_multiplier=-1))

        gmin_cols = sb("gmin_cols", [P, GJ], I32)
        dve.wait(got_grouped)
        have_gmin = dve.run(lambda e: e.tensor_reduce(
            gmin_cols[0:GP, :], grouped.rearrange("p (j n) -> p j n", j=GJ), AX.X, ALU.min))
        sp.wait(have_gmin)
        gmin_stored = sp.dma(lambda e: e.dma_start(gmin_d.rearrange("(p j) -> p j", j=GJ),
                                                   gmin_cols[0:GP, :]), ld_gmin)
        sp.wait(gmin_stored)
        got_gmin = sp.dma(lambda e: e.dma_start(
            gmin_sb[:, :], gmin_d.rearrange("(a g) -> a g", a=1).broadcast_to([P, GROUPS])), ld_gbc)

        pool.wait(have_gmin)
        acc_zeroed = pool.run(lambda e: e.memset(acc[:, :, :], 0.0))

        flag_f, flag_i, beyond = sb("flag_f", [P, 1]), sb("flag_i", [1, 1], I32), None

        def edge_lists():
            dve.wait(got_edges, got_gmin)
            gm = gmin_sb[:, :].unsqueeze(2).broadcast_to([P, GROUPS, GROUP])
            dve.chain(lambda e: e.tensor_tensor(
                rel_sb[:, :].rearrange("p (g j) -> p g j", j=GROUP),
                rel_sb[:, :].bitcast(I32).rearrange("p (g j) -> p g j", j=GROUP), gm, ALU.subtract))
            far = rows_sb[:, :, :].rearrange("p a b -> p (a b)")[:, 0:CHUNKS]
            dve.chain(lambda e: e.scalar_tensor_tensor(far, rel_sb[:, :], float(WIN), wgt_sb[:, :],
                                                       ALU.is_ge, ALU.mult))
            dve.chain(lambda e: e.tensor_single_scalar(far, far, 0.0, ALU.not_equal))
            flagged = dve.chain(lambda e: e.tensor_reduce(flag_f[:, :], far, AX.X, ALU.max))
            pe.wait(flagged, consts_ready)
            spread = pe.run(lambda e: e.matmul(psum[0][0:1, 0:P], flag_f[:, :], ident[:, :],
                                               start=True, stop=True))
            dve.wait(spread)
            dve.chain(lambda e: e.tensor_reduce(flag_f[0:1, :], psum[0][0:1, 0:P], AX.X, ALU.max))
            return dve.chain(lambda e: e.tensor_copy(flag_i[:, :], flag_f[0:1, :]))

        BA = 7
        A_SLOTS = 3
        xa = carve((A_SLOTS, BA, D), reset=0)
        stat6 = sb("stat6", [P, 2 * BA, 6])
        stat2 = sb("stat2", [P, 2 * BA, 2])
        std = sb("std", [P, 2 * BA])
        x_ld = [slot(f"x_ld{i}") for i in range(A_SLOTS)]
        xn_st = [slot(f"xn_st{i}") for i in range(A_SLOTS)]
        stats_zeroed = pool.run(lambda e: e.memset(stat2[:, :, :], 1.0))
        batches = [range(b, min(b + BA, T)) for b in range(0, T, BA)]

        def batch_dmas(tiles, dram, view, width):
            full = [t for t in tiles if rows(t) == P]
            if full:
                d = dram[full[0] * P:(full[-1] + 1) * P, :].rearrange("(t p) d -> p t d", p=P)
                yield view[:, 0:len(full), :], d
            if len(full) < len(tiles):
                t, n = tiles[-1], rows(tiles[-1])
                yield view[0:n, len(full), :], dram[t * P:t * P + n, :]

        xn_stored = {}
        loaded_a = {}

        def load_a(b):
            s = b % A_SLOTS
            if b >= A_SLOTS:
                sp.wait(xn_stored[b - A_SLOTS])
            for to, frm in batch_dmas(batches[b], x, xa[:, s], D):
                loaded_a[b] = sp.dma(lambda e, to=to, frm=frm: e.dma_start(to, frm), x_ld[s])

        for b in range(min(2, len(batches))):
            load_a(b)
        for b, tiles in enumerate(batches):
            if b + 2 < len(batches):
                load_a(b + 2)
            s, half = b % A_SLOTS, (b % 2) * BA
            n = len(tiles)
            dve.wait(loaded_a[b], stats_zeroed)
            for i, t in enumerate(tiles):
                r = rows(t)
                m = dve.run(lambda e, i=i, r=r, s=s, half=half: e.bn_stats(
                    stat6[0:r, half + i, :], xa[0:r, s, i, :]))
            dve.wait(m)
            for i, t in enumerate(tiles):
                r = rows(t)
                m = dve.run(lambda e, i=i, r=r, half=half: e.bn_aggr(
                    stat2[0:r, half + i, :], stat6[0:r, half + i, :]))
            act.wait(m)
            m = act.run(lambda e, half=half, n=n: e.activation(
                std[:, half:half + n], stat2[:, half:half + n, 1], ACT.Sqrt, bias=eps_sb[:, :]))
            dve.wait(m)
            dve.chain(lambda e, half=half, n=n: e.reciprocal(std[:, half:half + n], std[:, half:half + n]))
            for i, t in enumerate(tiles):
                r = rows(t)
                m = dve.run(lambda e, i=i, r=r, s=s, half=half: e.tensor_scalar(
                    xa[0:r, s, i, :], xa[0:r, s, i, :], stat2[0:r, half + i, 0:1],
                    std[0:r, half + i:half + i + 1], ALU.subtract, ALU.mult))
            act.wait(m)
            for frm, to in batch_dmas(tiles, xn_d, xa[:, s], D):
                xn_stored[b] = act.dma(lambda e, to=to, frm=frm: e.dma_start(to, frm), xn_st[s])
            if b == 0:
                flag_ready = edge_lists()
        all_xn_stored = [xn_stored[b] for b in range(max(0, len(batches) - A_SLOTS), len(batches))]

        taken[0] = 0
        R1 = 5
        xb = carve((R1, D))
        xnt = carve((R1, H, P))
        kvn = carve((2, 2 * D))
        sq = carve((2, 2 * D))
        top_b = taken[0]
        wkv_sb = carve((H, 2 * D))
        bkv_sb = carve((2 * D,))[0:1, :]
        gam_sb = carve((2 * D,))
        bet_sb = carve((2 * D,))
        wsum = sb("wsum", [P, H, 2 * HEADS])
        weff = sb("weff", [P, H, D])
        beff = sb("beff", [P, H])
        w1m_sb = carve((H, D))
        wqt_sb = carve((H, D + 1))
        pt_sb = carve((H, D + 1))
        w2m_sb = sb("w2m_sb", [P, H, D])
        w1g_sb = sb("w1g_sb", [P, H, D])
        w2g_sb = sb("w2g_sb", [P, H, D])
        b2m_sb = sb("b2m_sb", [1, D])
        bg_sb = sb("bg_sb", [1, 2, D])
        b1m_sb = sb("b1m_sb", [P, H])
        kv_bd = carve((H, P))
        ss = sb("ss", [P, 2, 2 * HEADS])
        gate_sb = sb("gate_sb", [P, H, NE])
        gateb_sb = sb("gateb_sb", [P, NE])

        def halves(w):
            return w.rearrange("(h p) f -> p h f", p=P)

        def row(v):
            return v.rearrange("(a d) -> a d", a=1)

        def everywhere(v, n):
            return row(v).broadcast_to([P, n])

        wld, wld2 = slot("weights_ld"), slot("weights_ld_late")
        sp.wait(*all_xn_stored)
        early = [(wkv_sb[:, :, :], halves(wkv)), (bkv_sb[:, :], row(bkv)),
                 (gam_sb, everywhere(kv_gamma, 2 * D)), (bet_sb, everywhere(kv_beta, 2 * D))]
        late = [(w1m_sb, halves(mix_w1)), (wqt_sb, halves(wqt_bq)), (w2m_sb[:, :, :], halves(mix_w2)),
                (w1g_sb[:, :, :], halves(gnn_w1t)), (w2g_sb[:, :, :], halves(gnn_w2t)),
                (b2m_sb[:, :], row(mix_b2)), (bg_sb[:, 0, :], row(gnn_b1)), (bg_sb[:, 1, :], row(gnn_b2)),
                (b1m_sb[:, :], mix_b1), (gate_sb[:, :, :], halves(gate_w)),
                (gateb_sb[:, :], everywhere(gate_b, NE))]
        for to, frm in early:
            got_early = sp.dma(lambda e, to=to, frm=frm: e.dma_start(to, frm), wld)
        for to, frm in late:
            got_late = sp.dma(lambda e, to=to, frm=frm: e.dma_start(to, frm), wld2)

        def centre(w, sums):
            dve.chain(lambda e: e.tensor_reduce(sums, w.rearrange("p (h c) -> p h c", c=HEADC), AX.X, ALU.add))
            dve.chain(lambda e: e.tensor_single_scalar(sums, sums, 1.0 / HEADC, ALU.mult))
            return dve.chain(lambda e: e.tensor_tensor(
                w.rearrange("p (h c) -> p h c", c=HEADC), w.rearrange("p (h c) -> p h c", c=HEADC),
                sums.unsqueeze(2).broadcast_to([w.shape[0], 2 * HEADS, HEADC]), ALU.subtract))

        def centre_all():
            dve.wait(got_early)
            for h in range(H):
                centre(wkv_sb[:, h, :], wsum[:, h, :])
            return centre(bkv_sb[:, :], wsum[0:1, 0, :])

        row_ld = [slot(f"row_ld{i}") for i in range(ROW_SLOTS)]
        s_ready, group_mm, group_added, group_copied, group_turned = {}, {}, {}, {}, {}
        SUM_SLOTS = 3
        sums = sb("sums", [WIN, SUM_SLOTS, D])

        def build_s(k):
            g0, n = S_GROUPS * k, min(S_GROUPS, GROUPS - S_GROUPS * k)
            last_reader = g0 - S_GROUPS * (S_SLOTS - 1) - 1
            if k >= S_SLOTS:
                dve.wait(group_mm[last_reader])
            c0, c = g0 * GROUP, n * GROUP
            s = s_sb[:, k % S_SLOTS, 0:c, :]
            wide = [P, c, WIN]
            dve.chain(lambda e: e.tensor_tensor(
                s, rel_sb[:, c0:c0 + c].unsqueeze(2).broadcast_to(wide),
                iota_win[:, :].unsqueeze(1).broadcast_to(wide), ALU.is_equal))
            m = dve.run(lambda e: e.tensor_tensor(
                s, s, wgt_sb[:, c0:c0 + c].unsqueeze(2).broadcast_to(wide), ALU.mult))
            for g in range(g0, g0 + n):
                s_ready[g] = m

        def gather_group(g):
            for c in range(g * GROUP, (g + 1) * GROUP):
                if g >= ROW_SLOTS // GROUP:
                    pool.wait(group_mm[g - ROW_SLOTS // GROUP])
                pool.dma(lambda e, c=c: e.indirect_dma_start(
                    out=rows_sb[:, c % ROW_SLOTS, :], out_offset=None, in_=xn_d,
                    in_offset=bass.IndirectOffsetOnAxis(ap=src_sb[:, c:c + 1], axis=0)),
                    row_ld[c % ROW_SLOTS])

        def multiply_group(g):
            pe.wait(s_ready[g])
            for j in range(GROUP):
                c = g * GROUP + j
                pe.wait((row_ld[c % ROW_SLOTS][0], 16 * (c // ROW_SLOTS + 1)))
            if g >= 2:
                pe.wait(group_copied[g - 2])
            k, j0 = g // S_GROUPS, (g % S_GROUPS) * GROUP
            for j in range(GROUP):
                c = g * GROUP + j
                m = pe.run(lambda e, j=j, c=c: e.matmul(
                    psum[g % 2][0:WIN, 0:D], s_sb[:, k % S_SLOTS, j0 + j, :], rows_sb[:, c % ROW_SLOTS, :],
                    start=j == 0, stop=j == GROUP - 1), tell=j == GROUP - 1)
            group_mm[g] = m
            act.wait(m)
            if g >= SUM_SLOTS:
                act.wait(group_turned[g - SUM_SLOTS])
            group_copied[g] = act.run(lambda e: e.copy(sums[0:WIN, g % SUM_SLOTS, :], psum[g % 2][0:WIN, 0:D]))

        def turn_group(g):
            pe.wait(group_copied[g])
            if g:
                pe.wait(group_added[g - 1])
            for h in range(H):
                m = pe.run(lambda e, h=h: e.transpose(
                    psum[7][:, h * WIN:(h + 1) * WIN], sums[0:WIN, g % SUM_SLOTS, h * P:(h + 1) * P],
                    ident[0:WIN, 0:WIN]), tell=h == H - 1)
            group_turned[g] = m

        def add_group(g):
            dve.wait(group_turned[g])

            def step(e):
                at = e.value_load(gmin_sb[0:1, g:g + 1], min_val=0, max_val=N - 1)
                win = acc[:, :, bass.ds(at, WIN)]
                return e.tensor_tensor(win, win, psum[7][:, 0:H * WIN].rearrange(
                    "p (h w) -> p h w", h=H), ALU.add)
            group_added[g] = dve.chain(step)

        xn_ld = [slot(f"xn_ld{i}") for i in range(R1)]
        xnt_st = [slot(f"xnt_st{i}") for i in range(R1)]
        xb_free, xnt_stored, kv_read, kvn_read, sq_read, tr_read = {}, {}, {}, {}, {}, {}
        state = {}

        def node_kv(t):
            r, s, par = rows(t), t % R1, t % 2
            if t >= R1:
                sp.wait(xb_free[t - R1])
            loaded = sp.dma(lambda e: e.dma_start(xb[0:r, s, :], xn_d[t * P:t * P + r, :]), xn_ld[s])
            yield
            pe.wait(loaded, consts_ready)
            if t >= 1:
                pe.wait(tr_read[t - 1])
            for h in range(H):
                m = pe.run(lambda e, h=h: e.transpose(psum[4][:, h * P:h * P + r],
                                                      xb[0:r, s, h * P:(h + 1) * P], ident[0:r, 0:r]),
                           tell=h == H - 1)
            xb_free[t] = m
            act.wait(m)
            if t >= R1:
                act.wait(xnt_stored[t - R1])
                act.wait(kv_read[t - R1])
            tr_read[t] = act.run(lambda e: e.copy(
                xnt[:, s, :, 0:r], psum[4][:, 0:H * P].rearrange("p (h n) -> p h n", h=H)[:, :, 0:r]))
            yield
            sp.wait(tr_read[t])
            xnt_stored[t] = sp.dma(lambda e: e.dma_start(
                xnt_d[:, :, t * P:t * P + r].rearrange("h p n -> p h n"), xnt[:, s, :, 0:r]), xnt_st[s])
            pe.wait(state["centred"], tr_read[t])
            if t >= 2:
                pe.wait(kvn_read[t - 2, "psum"])
            kv = psum[2 + par]
            pe.run(lambda e: e.matmul(kv[0:r, :], ones[0:1, 0:r], bkv_sb[:, :], start=True, stop=False), tell=False)
            for h in range(H):
                m = pe.run(lambda e, h=h: e.matmul(kv[0:r, :], xnt[:, s, h, 0:r], wkv_sb[:, h, :],
                                                   start=False, stop=h == H - 1), tell=h == H - 1)
            kv_read[t] = m
            act.wait(m)
            if t >= 2:
                act.wait(sq_read[t - 2])
            squared = act.run(lambda e: e.activation(sq[0:r, par, :], kv[0:r, :], ACT.Square))
            yield
            dve.wait(squared)
            sq_read[t] = dve.run(lambda e: e.tensor_reduce(
                ss[0:r, par, :], sq[0:r, par, :].rearrange("p (h c) -> p h c", c=HEADC), AX.X, ALU.add))
            act.wait(sq_read[t])
            rooted = act.run(lambda e: e.activation(ss[0:r, par, :], ss[0:r, par, :], ACT.Sqrt,
                                                    bias=eps_sb[0:r, :], scale=1.0 / HEADC))
            yield
            dve.wait(rooted)
            dve.chain(lambda e: e.reciprocal(ss[0:r, par, :], ss[0:r, par, :]))
            if t >= 2:
                dve.wait(kvn_read[t - 2])
            kvn_read[t, "psum"] = dve.chain(lambda e: e.tensor_tensor(
                kvn[0:r, par, :].rearrange("p (h c) -> p h c", c=HEADC),
                kv[0:r, :].rearrange("p (h c) -> p h c", c=HEADC),
                ss[0:r, par, :].unsqueeze(2).broadcast_to([r, 2 * HEADS, HEADC]), ALU.mult))
            dve.chain(lambda e: e.tensor_tensor(kvn[0:r, par, :], kvn[0:r, par, :], gam_sb[0:r, :], ALU.mult))
            m = dve.run(lambda e: e.tensor_tensor(kvn[0:r, par, :], kvn[0:r, par, :], bet_sb[0:r, :], ALU.add))
            yield
            pe.wait(m)
            for h in range(H):
                m = pe.run(lambda e, h=h: e.matmul(
                    psum[5 + h][:, 0:P], kvn[0:r, par, h * P:(h + 1) * P],
                    kvn[0:r, par, D + h * P:D + (h + 1) * P], start=t == 0, stop=t == T - 1),
                    tell=h == H - 1)
            kvn_read[t] = m

        def fold():
            z = dve.chain(lambda e: e.memset(kv_bd, 0.0))
            dve.wait(kvn_read[T - 1])
            for h in range(H):
                for q in range(P // HEADC):
                    a, b = q * HEADC, (q + 1) * HEADC
                    m = dve.run(lambda e, h=h, a=a, b=b: e.tensor_single_scalar(
                        kv_bd[a:b, h, a:b], psum[5 + h][a:b, a:b], 1.0 / N, ALU.mult))
            yield
            pe.wait(m, got_late)
            for h in range(H):
                m = pe.run(lambda e, h=h: e.matmul(psum[2 + h][:, 0:D + 1], kv_bd[:, h, :], wqt_sb[:, h, :],
                                                   start=True, stop=True))
            dve.wait(m)
            for h in range(H):
                dve.chain(lambda e, h=h: e.tensor_copy(pt_sb[:, h, :], psum[2 + h][:, 0:D + 1]))
                m = dve.chain(lambda e, h=h: e.tensor_tensor(pt_sb[:, h, h * P:(h + 1) * P],
                                                             pt_sb[:, h, h * P:(h + 1) * P], ident[:, :], ALU.add))
            m2 = dve.chain(lambda e: e.tensor_tensor(bg_sb[:, 0, :], bg_sb[:, 0, :], bg_sb[:, 1, :], ALU.add))
            yield
            pe.wait(m, m2)
            for i in range(H):
                for h in range(H):
                    pe.run(lambda e, i=i, h=h: e.matmul(psum[4 + i][:, 0:D], pt_sb[:, h, i * P:(i + 1) * P],
                                                        w1m_sb[:, h, :], start=h == 0, stop=h == H - 1), tell=False)
            for i in range(H):
                for h in range(H):
                    m = pe.run(lambda e, i=i, h=h: e.matmul(
                        psum[2 + i][:, 0:1], w1m_sb[:, h, i * P:(i + 1) * P], pt_sb[:, h, D:D + 1],
                        start=h == 0, stop=h == H - 1))
            dve.wait(m)
            for i in range(H):
                dve.run(lambda e, i=i: e.tensor_copy(weff[:, i, :], psum[4 + i][:, 0:D]))
                m = dve.run(lambda e, i=i: e.tensor_tensor(beff[:, i:i + 1], psum[2 + i][:, 0:1],
                                                           b1m_sb[:, i:i + 1], ALU.add))
            state["folded"] = m
            yield

        Q = 4
        UNITS = -(-T // Q)
        save = taken[0]
        taken[0] = 0
        xq = carve((2, H, Q * P))
        hq = carve((2, H, Q * P))
        RO = 4
        xr = carve((RO, 2, D))
        ego_o = carve((RO, D))
        base_o = carve((RO, D))
        top_b2 = taken[0]
        xq_ld = [slot(f"xq_ld{i}") for i in range(2)]
        xr_ld = [slot(f"xr_ld{i}") for i in range(RO)]
        out_st = [slot(f"be_st{i}") for i in range(RO)]
        xq_read, hq_read, ht_read, mix_read, be_stored, base_made = {}, {}, {}, {}, {}, {}

        have_rows = {}

        def load_rows(t):
            r, o = rows(t), t % RO
            if t >= RO:
                sp.wait(base_made[t - RO])
            sp.dma(lambda e: e.dma_start(xr[0:r, o, 0, :], x[t * P:t * P + r, :]), xr_ld[o])
            have_rows[t] = sp.dma(lambda e: e.dma_start(xr[0:r, o, 1, :], xn_d[t * P:t * P + r, :]), xr_ld[o])

        def node_mix(u):
            tiles = range(u * Q, min(u * Q + Q, T))
            n = sum(rows(t) for t in tiles)
            s = u % 2
            if u == 0:
                sp.wait(state["folded"], *[xnt_stored[t] for t in range(max(0, T - R1), T)])
                load_rows(0)
            if u >= 2:
                sp.wait(xq_read[u - 2])
            loaded = sp.dma(lambda e: e.dma_start(
                xq[:, s, :, 0:n], xnt_d[:, :, u * Q * P:u * Q * P + n].rearrange("h p n -> p h n")), xq_ld[s])
            yield
            pe.wait(loaded, state["folded"])
            if u >= 2:
                act.wait(hq_read[u - 2])
            for f in range(H):
                if (u, f) != (0, f):
                    pe.wait(ht_read[u - 1, f])
                for h in range(H):
                    m = pe.run(lambda e, f=f, h=h: e.matmul(
                        psum[2 + f][:, 0:n], weff[:, h, f * P:(f + 1) * P], xq[:, s, h, 0:n],
                        start=h == 0, stop=h == H - 1), tell=h == H - 1)
                act.wait(m)
                ht_read[u, f] = act.run(lambda e, f=f: e.activation(
                    hq[:, s, f, 0:n], psum[2 + f][:, 0:n], ACT.Gelu, bias=beff[:, f:f + 1]))
                yield
            for t in tiles:
                r, i, o, bank = rows(t), t - u * Q, t % RO, 4 + t % 2
                if t + 1 < T:
                    load_rows(t + 1)
                have = have_rows[t]
                pe.wait(ht_read[u, H - 1])
                if t >= 2:
                    pe.wait(*mix_read[t - 2])
                mix, ego = psum[bank][0:r, 0:D], psum[bank][0:r, D:2 * D]
                pe.run(lambda e, r=r, mix=mix: e.matmul(mix, ones[0:1, 0:r], b2m_sb[:, :], start=True, stop=False), tell=False)
                for f in range(H):
                    pe.run(lambda e, f=f, r=r, i=i, mix=mix: e.matmul(
                        mix, hq[:, s, f, i * P:i * P + r], w2m_sb[:, f, :], start=False, stop=f == H - 1), tell=False)
                pe.run(lambda e, r=r, ego=ego: e.matmul(ego, ones[0:1, 0:r], bg_sb[:, 0, :], start=True, stop=False), tell=False)
                for h in range(H):
                    m = pe.run(lambda e, h=h, r=r, i=i, ego=ego: e.matmul(
                        ego, xq[:, s, h, i * P:i * P + r], w1g_sb[:, h, :], start=False, stop=h == H - 1),
                        tell=h == H - 1)
                act.wait(m)
                if t >= RO:
                    act.wait(be_stored[t - RO])
                    dve.wait(be_stored[t - RO])
                a = act.run(lambda e, r=r, o=o, ego=ego: e.copy(ego_o[0:r, o, :], ego))
                dve.wait(m, have, a)
                d = dve.chain(lambda e, r=r, o=o, mix=mix: e.tensor_tensor(
                    base_o[0:r, o, :], mix, xr[0:r, o, 1, :], ALU.add))
                mix_read[t] = (a, d)
                d2 = dve.run(lambda e, r=r, o=o: e.tensor_tensor(
                    base_o[0:r, o, :], base_o[0:r, o, :], xr[0:r, o, 0, :], ALU.add))
                base_made[t] = d2
                act.wait(d2)
                act.dma(lambda e, t=t, r=r, o=o: e.dma_start(ego_d[t * P:t * P + r, :], ego_o[0:r, o, :]), out_st[o])
                be_stored[t] = act.dma(lambda e, t=t, r=r, o=o: e.dma_start(
                    base_d[t * P:t * P + r, :], base_o[0:r, o, :]), out_st[o])
                yield
            xq_read[u] = m
            hq_read[u] = m

        taken[0] = save

        def nodes_of_b():
            yield from run_skewed((node_kv(t) for t in range(T)), None)
            yield from fold()
            unit = node_mix(0)
            next(unit)
            for u in range(UNITS):
                ahead = node_mix(u + 1) if u + 1 < UNITS else None
                for piece, _ in enumerate(unit):
                    if piece == H + 1 and ahead:
                        next(ahead)
                        yield
                        continue
                    yield
                unit = ahead

        state["centred"] = centre_all()
        pool.wait(*all_xn_stored, acc_zeroed, got_edges, flag_ready)
        dve.wait(acc_zeroed)
        total = T + 5 + 3 + UNITS * H + T
        side = nodes_of_b()
        done_ticks = 0
        build_s(0)
        for g in range(GROUPS):
            gather_group(g)
            if g % S_GROUPS == 0 and g + S_GROUPS < GROUPS:
                build_s(g // S_GROUPS + 1)
            multiply_group(g)
            if g > 1:
                add_group(g - 2)
            if g:
                turn_group(g - 1)
            while done_ticks * (GROUPS - 4) < total * (g + 1):
                next(side, None)
                done_ticks += 1
        if GROUPS > 1:
            add_group(GROUPS - 2)
        turn_group(GROUPS - 1)
        add_group(GROUPS - 1)
        for _ in side:
            pass

        far_rows, far_s, far_sum, far_done = sem("far_rows"), sem("far_s"), sem("far_sum"), sem("far_done")
        far_dve, far_pool = sem("far_dve"), sem("far_pool")
        WIDE_SLOTS = 2
        far_idx = sb("far_idx", [P, 1], I32)
        far_w = sb("far_w", [P, 1])
        far_at = sb("far_at", [P, WIDE_WINDOWS])
        far_steps = sb("far_steps", [P, WIDE_WINDOWS])
        iota_wide = carve((WIDE,), reset=top_b2)
        s_wide = carve((WIDE_SLOTS, WIDE))
        row_buf = rows_sb[:, 0, :]
        groups_over = (group_mm[GROUPS - 1], group_added[GROUPS - 1])

        def far_pool_lane(e):
            flag = e.value_load(flag_i[:, :], min_val=0, max_val=1)
            with e.If(flag):
                e.iota(iota_wide, [[1, WIDE]], base=0, channel_multiplier=0,
                       allow_small_or_imprecise_dtypes=True).then_inc(far_pool, 1)
                e.iota(far_steps[:, :], [[-WIDE, WIDE_WINDOWS]], base=0, channel_multiplier=0,
                       allow_small_or_imprecise_dtypes=True).then_inc(far_pool, 1)
                with nc.Fori(0, CHUNKS, engines=[mybir.EngineType.Pool]) as c:
                    e.tensor_copy(far_idx[:, :], src_sb[:, bass.ds(c, 1)]).then_inc(far_done, 1)
                    e.wait_ge(far_done, 1)
                    e.sem_clear(far_done)
                    e.indirect_dma_start(out=row_buf, out_offset=None, in_=xn_d,
                                         in_offset=bass.IndirectOffsetOnAxis(ap=far_idx[:, :], axis=0)
                                         ).then_inc(far_rows, 16)
                    e.wait_ge(far_done, 1)
                    e.sem_clear(far_done)

        def far_pe_lane(e):
            flag = e.value_load(flag_i[:, :], min_val=0, max_val=1)
            with e.If(flag):
                with nc.Fori(0, CHUNKS, engines=[mybir.EngineType.PE]) as c:
                    e.wait_ge(far_rows, (c + 1) * 16)
                    for u in range(WIDE_WINDOWS):
                        e.wait_ge(far_s, u + 1)
                        if u == WIDE_WINDOWS - 1:
                            e.sem_clear(far_s)
                        for h in range(H):
                            m = e.matmul(psum[h][:, 0:WIDE], rows_sb[:, 0, h * P:(h + 1) * P],
                                         s_wide[:, u % WIDE_SLOTS, :], start=True, stop=True)
                        m.then_inc(far_sum, 1)

        def far_dve_lane(e):
            flag = e.value_load(flag_i[:, :], min_val=0, max_val=1)
            with e.If(flag):
                e.wait_ge(far_pool, 2)
                with nc.Fori(0, CHUNKS, engines=[mybir.EngineType.DVE]) as c:
                    step = [0]

                    def link(ins):
                        step[0] += 1
                        ins.then_inc(far_dve, 1)
                        e.wait_ge(far_dve, step[0])
                    link(e.scalar_tensor_tensor(far_w[:, :], rel_sb[:, bass.ds(c, 1)], float(WIN),
                                                wgt_sb[:, bass.ds(c, 1)], ALU.is_ge, ALU.mult))
                    link(e.tensor_tensor(far_at[:, 0:1], rel_sb[:, bass.ds(c, 1)], gmin_sb[:, bass.ds(c // GROUP, 1)], ALU.add))
                    link(e.tensor_scalar(far_at[:, 1:], far_steps[:, 1:], far_at[:, 0:1], None, ALU.add)
                         if WIDE_WINDOWS > 1 else e.tensor_copy(far_at[:, 0:1], far_at[:, 0:1]))
                    for u in range(WIDE_WINDOWS):
                        link(e.tensor_scalar(s_wide[:, u % WIDE_SLOTS, :], iota_wide, far_at[:, u:u + 1],
                                             far_w[:, :], ALU.is_equal, ALU.mult))
                        e.sem_inc(far_s, 1)
                        e.wait_ge(far_sum, u + 1)
                        for h in range(H):
                            win = acc[:, h, u * WIDE:(u + 1) * WIDE]
                            link(e.tensor_tensor(win, win, psum[h][:, 0:WIDE], ALU.add))
                    e.sem_clear(far_sum)
                    e.sem_clear(far_dve)
                    e.sem_inc(far_done, 1)

        for lane in (pool, pe, dve):
            lane.wait(flag_ready, *groups_over, *mix_read[T - 1])
        pool.run(far_pool_lane, tell=False)
        pe.run(far_pe_lane, tell=False)
        dve.run(far_dve_lane, tell=False)

        BC = 2
        C_UNITS = -(-T // BC)
        RC = 4
        taken[0] = 0
        xc = carve((RC, H, BC * P))
        ec = carve((RC, BC * D))
        bc = carve((RC, BC * D))
        comb = carve((RC, BC * 2 * D))
        junk = carve((BC * D,))
        h2t = carve((2, BC * H * P))
        top_c = taken[0]
        nrm = sb("nrm", [P, RC, 3, BC])
        c_ld = [slot(f"c_ld{i}") for i in range(RC)]
        c_st = [slot(f"c_st{i}") for i in range(RC)]
        mt_read, side_read, comb_stored, trc_read, logit_mm, ego_used, h2t_read, base_used = {}, {}, {}, {}, {}, {}, {}, {}
        TH = -(-T // 2)
        b_over = [be_stored[t] for t in range(max(0, T - RO), T)]

        def node_out(u):
            tiles = range(u * BC, min(u * BC + BC, T))
            nt, s, par = len(tiles), u % RC, u % 2
            n = sum(rows(t) for t in tiles)
            whole = all(rows(t) == P for t in tiles)
            if u == 0:
                sp.wait(*b_over)
            if u >= RC:
                sp.wait(mt_read[u - RC], comb_stored[u - RC], base_used[u - RC])
            sp.dma(lambda e: e.dma_start(
                xc[:, s, :, 0:n], xnt_d[:, :, u * BC * P:u * BC * P + n].rearrange("h p n -> p h n")), c_ld[s])
            for dram, buf in ((ego_d, ec), (base_d, bc)):
                view = buf[:, s, :].rearrange("p (t d) -> p t d", d=D)
                for to, frm in batch_dmas(list(tiles), dram, view, D):
                    loaded = sp.dma(lambda e, to=to, frm=frm: e.dma_start(to, frm), c_ld[s])
            yield
            dve.wait(loaded)
            summed = dve.run(lambda e: e.scalar_tensor_tensor(
                xc[:, s, :, 0:n], xc[:, s, :, 0:n], 1.0, acc[:, :, u * BC * P:u * BC * P + n],
                ALU.add, ALU.mult))
            state["acc_free"] = summed
            pe.wait(summed)
            if u >= 2:
                pe.wait(side_read[u - 2])
            for i, t in enumerate(tiles):
                r = rows(t)
                for h in range(H):
                    m = pe.run(lambda e, i=i, h=h, r=r: e.matmul(
                        psum[par][0:r, i * D:(i + 1) * D], xc[:, s, h, i * P:i * P + r], w2g_sb[:, h, :],
                        start=h == 0, stop=h == H - 1), tell=h == H - 1)
            mt_read[u] = m
            yield
            dve.wait(m)

            def pieces(view, width):
                if whole:
                    return [view[:, 0:nt * width]]
                return [view[0:rows(t), i * width:(i + 1) * width] for i, t in enumerate(tiles)]

            for o, ps in zip(pieces(ec[:, s, :], D), pieces(psum[par], D)):
                m = dve.run(lambda e, o=o, ps=ps: e.tensor_tensor(o, o, ps, ALU.add))
            side_read[u] = m
            dve.wait(m)
            for o in pieces(ec[:, s, :], D):
                m = dve.run(lambda e, o=o: e.scalar_tensor_tensor(o, o, LEAKY, o, ALU.mult, ALU.max))
            act.wait(m)
            for i, t in enumerate(tiles):
                r = rows(t)
                a = act.chain(lambda e, i=i, r=r: e.activation(
                    junk[0:r, i * D:(i + 1) * D], ec[0:r, s, i * D:(i + 1) * D], ACT.Square,
                    accum_out=nrm[0:r, s, 0, i:i + 1]))
            for i, t in enumerate(tiles) if not whole else [(0, None)]:
                v = nrm[:, s, 0, 0:nt] if whole else nrm[0:rows(t), s, 0, i:i + 1]
                a = act.run(lambda e, v=v: e.activation(v, v, ACT.Sqrt))
            yield
            dve.wait(a)
            for i, t in enumerate(tiles) if not whole else [(0, None)]:
                v = nrm[:, s, 0, 0:nt] if whole else nrm[0:rows(t), s, 0, i:i + 1]
                dve.chain(lambda e, v=v: e.tensor_single_scalar(v, v, NORM_EPS, ALU.max))
                dve.chain(lambda e, v=v: e.reciprocal(v, v))
            cview = comb[:, s, :].rearrange("p (t w d) -> p t w d", w=2, d=D)
            for i, t in enumerate(tiles):
                r = rows(t)
                m = dve.run(lambda e, i=i, r=r: e.scalar_tensor_tensor(
                    cview[0:r, i, 1, :], ec[0:r, s, i * D:(i + 1) * D], nrm[0:r, s, 0, i:i + 1],
                    bc[0:r, s, i * D:(i + 1) * D], ALU.mult, ALU.add))
            base_used[u] = m
            dve.wait(m)
            for i, t in enumerate(tiles):
                r = rows(t)
                m = dve.run(lambda e, i=i, r=r: e.bn_stats(stat6[0:r, par * BC + i, :], cview[0:r, i, 1, :]))
            dve.wait(m)
            for i, t in enumerate(tiles):
                r = rows(t)
                m = dve.run(lambda e, i=i, r=r: e.bn_aggr(stat2[0:r, par * BC + i, :], stat6[0:r, par * BC + i, :]))
            act.wait(m)
            a = act.run(lambda e: e.activation(std[:, par * BC:par * BC + nt],
                                               stat2[:, par * BC:par * BC + nt, 1], ACT.Sqrt, bias=eps_sb[:, :]))
            yield
            dve.wait(a)
            dve.chain(lambda e: e.reciprocal(std[:, par * BC:par * BC + nt], std[:, par * BC:par * BC + nt]))
            for i, t in enumerate(tiles):
                r = rows(t)
                m = dve.run(lambda e, i=i, r=r: e.tensor_scalar(
                    cview[0:r, i, 0, :], cview[0:r, i, 1, :], stat2[0:r, par * BC + i, 0:1],
                    std[0:r, par * BC + i:par * BC + i + 1], ALU.subtract, ALU.mult))
            normed = m
            act.wait(m)
            for i, t in enumerate(tiles):
                r = rows(t)
                act.dma(lambda e, i=i, t=t, r=r: e.dma_start(
                    comb_d[t * P:t * P + r, :], comb[0:r, s, i * 2 * D:(i + 1) * 2 * D]), c_st[s])
                comb_stored[u] = act.dma(lambda e, i=i, t=t, r=r: e.dma_start(
                    out[t * P:t * P + r, :], cview[0:r, i, 1, :]), c_st[s])
            pe.wait(normed)
            if u >= 2:
                pe.wait(trc_read[u - 2])
            for i, t in enumerate(tiles):
                r = rows(t)
                for h in range(H):
                    m = pe.run(lambda e, i=i, h=h, r=r: e.transpose(
                        psum[2 + par][:, (i * H + h) * P:(i * H + h) * P + r], cview[0:r, i, 0, h * P:(h + 1) * P],
                        ident[0:r, 0:r]), tell=h == H - 1)
            act.wait(m)
            if u >= 2:
                act.wait(logit_mm[u - 2])
            for i, t in enumerate(tiles):
                r = rows(t)
                a = act.run(lambda e, i=i, r=r: e.copy(
                    h2t[:, par, i * D:(i + 1) * D].rearrange("p (h n) -> p h n", h=H)[:, :, 0:r],
                    psum[2 + par][:, i * D:(i + 1) * D].rearrange("p (h n) -> p h n", h=H)[:, :, 0:r]))
            trc_read[u] = a
            yield
            pe.wait(a)
            for i, t in enumerate(tiles):
                r = rows(t)
                lg = psum[6 + t // TH][0:r, (t % TH) * NE:(t % TH + 1) * NE]
                for h in range(H):
                    m = pe.run(lambda e, i=i, h=h, r=r, lg=lg: e.matmul(
                        lg, h2t[:, par, (i * H + h) * P:(i * H + h) * P + r], gate_sb[:, h, :],
                        start=h == 0, stop=h == H - 1), tell=h == H - 1)
            logit_mm[u] = m

        for _ in run_skewed((node_out(u) for u in range(C_UNITS)), None):
            pass
        c_stored = [comb_stored[u] for u in range(max(0, C_UNITS - RC), C_UNITS)]

        flat = acc[:, :, :].rearrange("p h w -> p (h w)")
        behind = [ROUTE_AT]

        def route_buf(*shape):
            at, n = behind[0], math.prod(shape)
            behind[0] += n
            v = flat[:, at:at + n]
            return v if len(shape) == 1 else v.rearrange("p (a b) -> p a b", a=shape[0])
        lg, hot, tmp, tot = (route_buf(T, NE) for _ in range(4))
        c1 = route_buf(T)
        prb = route_buf(T)
        lo = route_buf(T)
        hi = route_buf(T)
        ids = route_buf(T)
        pos_i = route_buf(T).bitcast(I32)
        e_desc = sb("e_desc", [P, NE])
        e_base = sb("e_base", [P, NE])
        rl = rows(T - 1)

        def tall(v):
            return v.unsqueeze(2).broadcast_to([P, T, NE])

        def per_expert(v):
            return v.unsqueeze(1).broadcast_to([P, T, NE])

        pool.wait(state["acc_free"])
        dve.wait(state["acc_free"])
        pool.run(lambda e: e.iota(e_desc[:, :], [[-1, NE]], base=NE, channel_multiplier=0,
                                  allow_small_or_imprecise_dtypes=True))
        pool.run(lambda e: e.iota(e_base[:, :], [[SLOT_TILES, NE]], base=0, channel_multiplier=0,
                                  allow_small_or_imprecise_dtypes=True))
        ids_ready = pool.run(lambda e: e.iota(ids[:, :], [[P, T]], base=1, channel_multiplier=1,
                                              allow_small_or_imprecise_dtypes=True))
        dve.chain(lambda e: e.memset(lg[:, T - 1, :], 0.0))
        dve.wait(logit_mm[C_UNITS - 1], ids_ready)

        def logits_plus_bias(t0, t1, r):
            bank = psum[6 + t0 // TH][0:r, (t0 % TH) * NE:(t0 % TH + t1 - t0) * NE].rearrange(
                "p (t e) -> p t e", e=NE)
            return dve.run(lambda e: e.tensor_tensor(
                lg[0:r, t0:t1, :], bank, gateb_sb[0:r, :].unsqueeze(1).broadcast_to([r, t1 - t0, NE]), ALU.add))
        spans = [(0, min(TH, T - 1), P), (TH, T - 1, P), (T - 1, T, rl)]
        for t0, t1, r in spans:
            if t1 > t0:
                m = logits_plus_bias(t0, t1, r)
        dve.wait(m)
        dve.chain(lambda e: e.tensor_reduce(c1[:, :], lg, AX.X, ALU.max))
        m_shift = dve.chain(lambda e: e.tensor_tensor(lg, lg, tall(c1[:, :]), ALU.subtract))
        act.wait(m_shift)
        a = act.run(lambda e: e.activation(tmp, lg, ACT.Exp))
        dve.chain(lambda e: e.tensor_single_scalar(hot, lg, 0.0, ALU.is_equal))
        dve.chain(lambda e: e.tensor_tensor(hot, hot, per_expert(e_desc[:, :]), ALU.mult))
        dve.chain(lambda e: e.tensor_reduce(c1[:, :], hot, AX.X, ALU.max))
        dve.chain(lambda e: e.tensor_tensor(hot, hot, tall(c1[:, :]), ALU.is_equal))
        if rl < P:
            dve.chain(lambda e: e.tensor_copy(tot[:, T - 1, :], hot[:, T - 1, :]))
            dve.chain(lambda e: e.memset(hot[:, T - 1, :], 0.0))
            dve.chain(lambda e: e.tensor_copy(hot[0:rl, T - 1, :], tot[0:rl, T - 1, :]))
        hot_ready = dve.chain(lambda e: e.tensor_reduce(c1[:, :], hot, AX.X, ALU.max))
        dve.wait(a)
        dve.chain(lambda e: e.tensor_reduce(prb[:, :], tmp, AX.X, ALU.add))
        dve.chain(lambda e: e.reciprocal(prb[:, :], prb[:, :]))
        pe.wait(hot_ready)
        cuts = [(0, TH), (TH, T)]
        for k, (t0, t1) in enumerate(cuts):
            hv = hot[:, t0:t1, :].rearrange("p t e -> p (t e)")
            pe.run(lambda e, k=k, hv=hv: e.matmul(psum[k][:, 0:hv.shape[1]], upper[:, :], hv, start=True, stop=True))
            m = pe.run(lambda e, k=k, hv=hv: e.matmul(psum[2 + k][:, 0:hv.shape[1]], ones[:, :], hv, start=True, stop=True))
        dve.wait(m)
        for k, (t0, t1) in enumerate(cuts):
            w = (t1 - t0) * NE
            dve.run(lambda e, k=k, t0=t0, t1=t1, w=w: e.tensor_copy(
                tot[:, t0:t1, :].rearrange("p t e -> p (t e)"), psum[2 + k][:, 0:w]))
            m = dve.run(lambda e, k=k, t0=t0, t1=t1, w=w: e.tensor_copy(
                lg[:, t0:t1, :].rearrange("p t e -> p (t e)"), psum[k][:, 0:w]))
        zero = route_buf(T)
        m = dve.run(lambda e: e.memset(zero[:, :], 0.0))
        dve.wait(m)
        for x_ in range(NE):
            m = dve.run(lambda e, x_=x_: e.tensor_tensor_scan(tmp[:, :, x_], tot[:, :, x_], zero[:, :], 0.0,
                                                              ALU.add, ALU.add))
        dve.wait(m)
        dve.chain(lambda e: e.tensor_tensor(lg, lg, tmp, ALU.add))
        dve.chain(lambda e: e.tensor_tensor(lg, lg, tot, ALU.subtract))
        dve.chain(lambda e: e.tensor_tensor(lg, lg, hot, ALU.mult))
        dve.chain(lambda e: e.tensor_reduce(lo[:, :], lg, AX.X, ALU.add))
        dve.chain(lambda e: e.tensor_tensor(hot, hot, per_expert(e_base[:, :]), ALU.mult))
        dve.chain(lambda e: e.tensor_reduce(hi[:, :], hot, AX.X, ALU.add))
        dve.chain(lambda e: e.tensor_single_scalar(zero[:, :], lo[:, :], float(CAP), ALU.is_le))
        dve.chain(lambda e: e.tensor_tensor(zero[:, :], zero[:, :], c1[:, :], ALU.mult))
        dve.chain(lambda e: e.tensor_scalar(zero[:, :], zero[:, :], -1024.0, 1024.0, ALU.mult, ALU.add))
        dve.chain(lambda e: e.tensor_tensor(hi[:, :], hi[:, :], zero[:, :], ALU.add))
        dve.chain(lambda e: e.tensor_single_scalar(lo[:, :], lo[:, :], 1.0, ALU.subtract))
        dve.chain(lambda e: e.tensor_copy(pos_i[:, :], lo[:, :]))
        dve.chain(lambda e: e.tensor_single_scalar(pos_i[:, :], pos_i[:, :], P - 1, ALU.bitwise_and))
        dve.chain(lambda e: e.tensor_copy(c1[:, :], pos_i[:, :]))
        dve.chain(lambda e: e.tensor_tensor(lo[:, :], lo[:, :], c1[:, :], ALU.subtract))
        dve.chain(lambda e: e.tensor_single_scalar(lo[:, :], lo[:, :], 1.0 / P, ALU.mult))
        routed = dve.chain(lambda e: e.tensor_tensor(hi[:, :], hi[:, :], lo[:, :], ALU.add))

        at_row = route_buf(RT, P)
        at_col = route_buf(RT, 2 * TABLE)
        table_mm = {}
        for t in range(T):
            s = t % RT
            pool.wait(routed)
            if t >= RT:
                pool.wait(table_mm[t - RT])
                dve.wait(table_mm[t - RT])
            a = pool.run(lambda e, t=t, s=s: e.tensor_scalar(
                at_row[:, s, :], iota_p[:, :], c1[:, t:t + 1], None, ALU.is_equal))
            dve.run(lambda e, t=t, s=s: e.tensor_scalar(
                at_col[:, s, 0:TABLE], iota_p[:, 0:TABLE], hi[:, t:t + 1], ids[:, t:t + 1], ALU.is_equal, ALU.mult))
            d = dve.run(lambda e, t=t, s=s: e.tensor_scalar(
                at_col[:, s, TABLE:2 * TABLE], iota_p[:, 0:TABLE], hi[:, t:t + 1], prb[:, t:t + 1], ALU.is_equal, ALU.mult))
            pe.wait(a, d)
            table_mm[t] = pe.run(lambda e, t=t, s=s: e.matmul(
                psum[4][:, 0:2 * TABLE], at_row[:, s, :], at_col[:, s, :], start=t == 0, stop=t == T - 1))
        gat_i = sb("gat_i", [P, TABLE], I32)
        sca_i = sb("sca_i", [P, TABLE], I32)
        sprb = upper
        idf = route_buf(TABLE)
        empty = route_buf(TABLE)
        dve.wait(table_mm[T - 1])
        dve.chain(lambda e: e.tensor_copy(sprb[:, :], psum[4][:, TABLE:2 * TABLE]))
        dve.chain(lambda e: e.tensor_single_scalar(idf[:, :], psum[4][:, 0:TABLE], 1.0, ALU.subtract))
        dve.chain(lambda e: e.tensor_single_scalar(empty[:, :], idf[:, :], 0.0, ALU.is_lt))
        dve.chain(lambda e: e.scalar_tensor_tensor(empty[:, :], empty[:, :], float(2 * N), idf[:, :], ALU.mult, ALU.add))
        dve.chain(lambda e: e.tensor_copy(sca_i[:, :], empty[:, :]))
        dve.chain(lambda e: e.tensor_single_scalar(idf[:, :], idf[:, :], 0.0, ALU.max))
        table_ready = dve.chain(lambda e: e.tensor_copy(gat_i[:, :], idf[:, :]))

        U_E = -(-SLOT_TILES // GE)
        per_w = EXPERT_W - D
        WS = [flat[:, i * EXPERT_W:(i + 1) * EXPERT_W] for i in range(2)]
        hts = [flat[:, 2 * EXPERT_W + i * FC * GE * P:2 * EXPERT_W + (i + 1) * FC * GE * P] for i in range(2)]
        taken[0] = 0
        RX = 3 * GE
        xs = carve((RX, 2 * D))
        xgt = carve((2, H, GE * P))
        yo = carve((4, D))
        mk = carve((2, D))
        fb1 = sb("fb1", [P, NE, FC])
        big = sb("big", [P, 1])
        nbig = sb("nbig", [P, 1])
        nil = sb("nil", [P, 1])
        w_ld = [slot(f"w_ld{i}") for i in range(2)]
        xs_ld = [slot(f"xs_ld{i}") for i in range(RX)]
        y_st = [slot(f"y_st{i}") for i in range(4)]
        dve.run(lambda e: e.memset(big[:, :], 10000.0))
        dve.run(lambda e: e.memset(nbig[:, :], -10000.0))
        consts_e = dve.run(lambda e: e.memset(nil[:, :], 0.0))
        dve.wait(consts_e)
        weights_ready, unit_read, xs_free, tre_read, xgt_read, ht_full = {}, {}, {}, {}, {}, {}
        relu_read, y_read, y_stored, biased = {}, {}, {}, {}
        c_readers = (logit_mm[C_UNITS - 1], side_read[C_UNITS - 1], table_ready)
        units = [(x_, j) for x_ in range(NE) for j in range(U_E)]
        tr_n, s1_n, y_n = [0], [0], [0]

        def w1v(x_):
            return WS[x_ % 2][:, 0:H * FF].rearrange("p (h f) -> p h f", h=H)

        def w2v(x_):
            return WS[x_ % 2][:, H * FF:per_w].rearrange("p (c d) -> p c d", c=FC)

        def expert_unit(k):
            x_, j = units[k]
            a0, a1 = j * GE, min(j * GE + GE, SLOT_TILES)
            sizes = [min(P, CAP - a * P) for a in range(a0, a1)]
            n, par = sum(sizes), k % 2
            if j == 0:
                if k == 0:
                    sp.wait(*c_readers, *c_stored)
                    sp.dma(lambda e: e.dma_start(fb1[:, :, :], ffn_b1), w_ld[0])
                if x_ >= 2:
                    sp.wait(unit_read[U_E * (x_ - 1) - 1], biased[U_E * (x_ - 1) - 1])
                sp.dma(lambda e: e.dma_start(w1v(x_), ffn_w1[x_].rearrange("(h p) f -> p h f", p=P)), w_ld[x_ % 2])
                sp.dma(lambda e: e.dma_start(w2v(x_), ffn_w2[x_].rearrange("(c p) d -> p c d", p=P)), w_ld[x_ % 2])
                weights_ready[x_] = sp.dma(lambda e: e.dma_start(
                    WS[x_ % 2][:, per_w:per_w + D], ffn_b2[x_:x_ + 1, :].broadcast_to([P, D])), w_ld[x_ % 2])
            if k == 0:
                pool.wait(*c_readers, *c_stored)
            got = []
            for i, r in enumerate(sizes):
                s, col = (k * GE + i) % RX, x_ * SLOT_TILES + a0 + i
                if (k * GE + i) - RX in xs_free:
                    pool.wait(xs_free[k * GE + i - RX])
                got.append(pool.dma(lambda e, s=s, col=col, r=r: e.indirect_dma_start(
                    out=xs[0:r, s, :], out_offset=None, in_=comb_d,
                    in_offset=bass.IndirectOffsetOnAxis(ap=gat_i[0:r, col:col + 1], axis=0)), xs_ld[s]))
            yield
            for i, r in enumerate(sizes):
                s, bank = (k * GE + i) % RX, tr_n[0] % 2
                pe.wait(got[i])
                if tr_n[0] >= 2:
                    pe.wait(tre_read[tr_n[0] - 2])
                for h in range(H):
                    m = pe.run(lambda e, h=h, s=s, r=r, bank=bank: e.transpose(
                        psum[bank][:, h * P:h * P + r], xs[0:r, s, h * P:(h + 1) * P], ident[0:r, 0:r]),
                        tell=h == H - 1)
                act.wait(m)
                if k >= 2:
                    act.wait(xgt_read[k - 2])
                a = act.run(lambda e, i=i, r=r, bank=bank: e.copy(
                    xgt[:, par, :, i * P:i * P + r],
                    psum[bank][:, 0:H * P].rearrange("p (h n) -> p h n", h=H)[:, :, 0:r]))
                tre_read[tr_n[0]] = a
                tr_n[0] += 1
            yield
            pe.wait(a, weights_ready[x_])
            if k >= 2:
                act.wait(unit_read[k - 2])
            act.wait(weights_ready[0])
            for f in range(FC):
                bank = 2 + s1_n[0] % 3
                if s1_n[0] >= 3:
                    pe.wait(relu_read[s1_n[0] - 3])
                for h in range(H):
                    m = pe.run(lambda e, f=f, h=h, bank=bank: e.matmul(
                        psum[bank][:, 0:n], w1v(x_)[:, h, f * P:(f + 1) * P], xgt[:, par, h, 0:n],
                        start=h == 0, stop=h == H - 1), tell=h == H - 1)
                act.wait(m)
                relu_read[s1_n[0]] = act.run(lambda e, f=f, bank=bank: e.activation(
                    hts[par][:, f * GE * P:f * GE * P + n], psum[bank][:, 0:n], ACT.Relu, bias=fb1[:, x_, f:f + 1]))
                s1_n[0] += 1
            xgt_read[k] = m
            hidden = relu_read[s1_n[0] - 1]
            yield
            pe.wait(hidden)
            dve.wait(weights_ready[x_])
            for i, r in enumerate(sizes):
                s, col = (k * GE + i) % RX, x_ * SLOT_TILES + a0 + i
                q = y_n[0]
                bank, o = 5 + q % 3, q % 4
                if q >= 3:
                    pe.wait(y_read[q - 3])
                for f in range(FC):
                    m = pe.run(lambda e, f=f, i=i, r=r, bank=bank: e.matmul(
                        psum[bank][0:r, 0:D], hts[par][:, f * GE * P + i * P:f * GE * P + i * P + r],
                        w2v(x_)[:, f, :], start=f == 0, stop=f == FC - 1), tell=f == FC - 1)
                dve.wait(m)
                if q >= 4:
                    dve.wait(y_stored[q - 4])
                y, b2 = yo[0:r, o, :], WS[x_ % 2][0:r, per_w:per_w + D]
                y_read[q] = dve.chain(lambda e, y=y, b2=b2, r=r, bank=bank: e.tensor_tensor(
                    y, psum[bank][0:r, 0:D], b2, ALU.add))
                dve.chain(lambda e, y=y, r=r, col=col: e.tensor_scalar(y, y, sprb[0:r, col:col + 1], None, ALU.mult))
                mask = mk[0:r, q % 2, :].bitcast(I32)
                for make, value in (
                        (lambda e, y=y, mask=mask: e.tensor_tensor(mask, y, y, ALU.not_equal), nil),
                        (lambda e, y=y, mask=mask: e.tensor_single_scalar(mask, y, math.inf, ALU.is_equal), big),
                        (lambda e, y=y, mask=mask: e.tensor_single_scalar(mask, y, -math.inf, ALU.is_equal), nbig)):
                    dve.chain(make)
                    dve.chain(lambda e, y=y, mask=mask, value=value, r=r: e.copy_predicated(
                        y, mask, value[0:r, :].broadcast_to([r, D])))
                m2 = dve.run(lambda e, y=y, s=s, r=r: e.tensor_tensor(y, y, xs[0:r, s, D:2 * D], ALU.add))
                xs_free[k * GE + i] = m2
                pool.wait(m2)
                y_stored[q] = pool.dma(lambda e, y=y, r=r, col=col: e.indirect_dma_start(
                    out=out, out_offset=bass.IndirectOffsetOnAxis(ap=sca_i[0:r, col:col + 1], axis=0),
                    in_=y, in_offset=None, bounds_check=N - 1, oob_is_err=False), y_st[o])
                y_n[0] += 1
            unit_read[k], biased[k] = m, y_read[y_n[0] - 1]

        for _ in run_skewed((expert_unit(k) for k in range(len(units))), None):
            pass
        for q in range(max(0, y_n[0] - 4), y_n[0]):
            pool.wait(y_stored[q])
        sp.wait(*c_stored)

        block = ctx.enter_context(nc.Block())
        block.sync(sp.play)
        block.gpsimd(pool.play)
        block.tensor(pe.play)
        block.vector(dve.play)
        block.scalar(act.play)


def kernel(**inputs):
    import numpy as np
    import concourse.bacc as bacc
    from concourse import mybir as my
    from concourse.bass_utils import run_bass_kernel_spmd

    given = {k: np.ascontiguousarray(v) for k, v in inputs.items()}
    n, d = given["x"].shape
    edges = given["src"].shape[0]
    unit = GROUP * P
    groups = -(-edges // unit)

    def padded(a, fill):
        whole = np.full(groups * unit, fill, a.dtype)
        whole[:edges] = a
        return whole

    def columns(a):
        return np.ascontiguousarray(a.reshape(groups * GROUP, P).T)

    per_row = next(k for k in range(-(-groups // P), groups + 1) if groups % k == 0)
    dst = padded(given["dst"], n)
    heads = d // HEADC
    w = given["L0_mix_w_qkv"].reshape(d, heads, 3, HEADC)
    b = given["L0_mix_b_qkv"].reshape(heads, 3, HEADC)

    def twice(name):
        return np.concatenate([np.tile(given[f"L0_mix_kln_{name}"], heads), np.tile(given[f"L0_mix_vln_{name}"], heads)])

    def by_partition(v):
        return np.ascontiguousarray(v.reshape(-1, P).T)

    b1 = given["L0_ffn_b1"]
    arrays = {
        "x": given["x"],
        "src": columns(padded(given["src"], 0)), "dst": columns(dst),
        "weight": columns(padded(given["edge_weight"], 0)),
        "dst_grouped": dst.reshape(groups // per_row, per_row * unit),
        "gnn_w1t": given["L0_gnn_W1"].T, "gnn_b1": given["L0_gnn_b1"],
        "gnn_w2t": given["L0_gnn_W2"].T, "gnn_b2": given["L0_gnn_b2"],
        "wqt_bq": np.concatenate([w[:, :, 0].reshape(d, d).T, b[:, 0].reshape(d, 1)], axis=1),
        "wkv": np.concatenate([w[:, :, 1].reshape(d, d), w[:, :, 2].reshape(d, d)], axis=1),
        "bkv": np.concatenate([b[:, 1].reshape(d), b[:, 2].reshape(d)]),
        "kv_gamma": twice("g"), "kv_beta": twice("b"),
        "mix_w1": given["L0_mix_w1"], "mix_b1": by_partition(given["L0_mix_b1"]),
        "mix_w2": given["L0_mix_w2"], "mix_b2": given["L0_mix_b2"],
        "gate_w": given["L0_ffn_gate_w"], "gate_b": given["L0_ffn_gate_b"],
        "ffn_w1": given["L0_ffn_w1"],
        "ffn_b1": b1.reshape(b1.shape[0], -1, P).transpose(2, 0, 1),
        "ffn_w2": given["L0_ffn_w2"], "ffn_b2": given["L0_ffn_b2"],
    }
    nc = bacc.Bacc("TRN2", target_bir_lowering=False, num_devices=1)
    feeds, args = {}, []
    for name, a in arrays.items():
        a = np.ascontiguousarray(a)
        feeds[f"{name}_in"] = a
        args.append(nc.dram_tensor(f"{name}_in", a.shape, my.dt.from_np(a.dtype), kind="ExternalInput").ap())
    args.append(nc.dram_tensor("out_dram", (n, d), my.dt.float32, kind="ExternalOutput").ap())
    build(nc, *args)
    ran = run_bass_kernel_spmd(nc, [feeds], core_ids=[0])
    return ran.results[0]["out_dram"]
```

```python
import math
from contextlib import ExitStack

import concourse.bass as bass
from concourse import mybir

F32 = mybir.dt.float32
F32R = mybir.dt.float32r
I32 = mybir.dt.int32
ALU = mybir.AluOpType
ACT = mybir.ActivationFunctionType
AX = mybir.AxisListType

P = 128
GROUP = 4
WIN = 48
WIDE = 500
EPS = 1e-5
NORM_EPS = 1e-12
LEAKY = 0.2
HEADC = 32
CAPACITY_FACTOR = 1.25


class Lane:

    def __init__(self, done):
        self.done, self.count, self.steps, self.waited = done, 0, [], {}

    def wait(self, *marks):
        for sem, value in marks:
            if self.waited.get(sem, 0) < value:
                self.waited[sem] = value
                self.steps.append(lambda e, s=sem, v=value: e.wait_ge(s, v))

    def run(self, step, tell=True):
        if not tell:
            self.steps.append(step)
            return None
        self.count += 1
        self.steps.append(lambda e: step(e).then_inc(self.done, 1))
        return self.done, self.count

    def chain(self, step):
        mark = self.run(step)
        self.wait(mark)
        return mark

    def dma(self, step, slot):
        slot[1] += 16
        self.steps.append(lambda e, s=slot[0]: step(e).then_inc(s, 16))
        return slot[0], slot[1]

    def play(self, engine):
        for step in self.steps:
            step(engine)


def run_skewed(pipeline, youngest_first=False):
    live = []

    def advance():
        order = live[::-1] if youngest_first else live
        ended = [u for u in order if next(u, "end") == "end"]
        live[:] = [u for u in live if u not in ended]

    for unit in pipeline:
        live.append(unit)
        advance()
        yield
    while live:
        advance()
        yield


def build(nc, x, src, dst, weight, dst_grouped, gnn_w1t, gnn_b1, gnn_w2t, gnn_b2,
          wqt_bq, wkv, bkv, kv_gamma, kv_beta, mix_w1, mix_b1, mix_w2, mix_b2,
          gate_w, gate_b, ffn_w1, ffn_b1, ffn_w2, ffn_b2, out):
    N, D = x.shape
    H = D // P
    T = -(-N // P)
    GROUPS = src.shape[1] // GROUP
    CHUNKS = src.shape[1]
    NE = gate_w.shape[1]
    FF = ffn_w1.shape[2]
    FC = FF // P
    CAP = max(1, math.ceil(CAPACITY_FACTOR * N / NE))
    SLOT_TILES = -(-CAP // P)
    TABLE = NE * SLOT_TILES
    WIDE_WINDOWS = -(-N // WIDE)
    ACC_W = max(WIDE_WINDOWS * WIDE, T * P, N + WIN)
    GE = 4
    EXPERT_W = H * FF + FC * D
    HID_W = FC * GE * P
    RT = 6
    ROUTE_W = 4 * T * NE + 7 * T + (3 * RT + 2) * P
    ACC_W = max(ACC_W, -(-(3 * EXPERT_W + ROUTE_W) // H))
    HEADS = D // HEADC
    GP, GJ = dst_grouped.shape[0], dst_grouped.shape[1] // (GROUP * P)
    assert GP * GJ == GROUPS and TABLE <= P and D == 2 * P

    def rows(t):
        return min(P, N - t * P)

    ctx = ExitStack()
    before_e = ExitStack()
    with ctx:
        def sb(name, shape, dt=F32):
            return ctx.enter_context(nc.sbuf_tensor(name, shape, dt))

        def sem(name):
            return ctx.enter_context(nc.semaphore(name))

        def slot(name):
            return [sem(name), 0]

        xn_d = nc.dram_tensor("xn_scratch", [N, D], F32).ap()
        xnt_d = nc.dram_tensor("xnt_scratch", [H, P, T * P], F32).ap()
        base_d = nc.dram_tensor("base_scratch", [N, D], F32).ap()
        ego_d = nc.dram_tensor("ego_scratch", [N, D], F32).ap()
        h2_d = nc.dram_tensor("h2_scratch", [N, D], F32).ap()
        gmin_d = nc.dram_tensor("group_min_scratch", [GROUPS], I32).ap()

        acc = before_e.enter_context(nc.sbuf_tensor("acc", [P, H, ACC_W], F32, side="right"))
        src_sb = sb("src_sb", [P, CHUNKS], I32)
        rel_sb = sb("rel_sb", [P, CHUNKS])
        wgt_sb = sb("wgt_sb", [P, CHUNKS])
        gmin_sb = sb("gmin_sb", [P, GROUPS], I32)
        iota_win = sb("iota_win", [P, WIN])
        iota_p = sb("iota_p", [P, P])
        ident = sb("ident", [P, P])
        upper = sb("upper", [P, P])
        ones = sb("ones", [P, P])
        eps_sb = sb("eps_sb", [P, 1])
        ROW_SLOTS = 4 * GROUP
        rows_sb = sb("rows_sb", [P, ROW_SLOTS, D])
        S_SLOTS, S_GROUPS = 3, 2
        s_sb = sb("s_sb", [P, S_SLOTS, S_GROUPS * GROUP, WIN])
        ARENA = 12 * 1024
        arena = before_e.enter_context(nc.sbuf_tensor("arena", [P, ARENA], F32, side="right"))

        psum = [ctx.enter_context(nc.psum_tensor(f"bank{i}", [P, 512], F32)) for i in range(8)]

        sp, pool, pe, dve, act = (Lane(sem(f"done_{n}")) for n in ("sp", "pool", "pe", "dve", "act"))

        taken = [0]

        def carve(shape, reset=None):
            if reset is not None:
                taken[0] = reset
            n = math.prod(shape)
            at = taken[0]
            taken[0] += n
            assert taken[0] <= ARENA, (taken[0], ARENA)
            v = arena[:, at:at + n]
            if len(shape) == 2:
                v = v.rearrange("p (a b) -> p a b", a=shape[0])
            elif len(shape) == 3:
                v = v.rearrange("p (a b c) -> p a b c", a=shape[0], b=shape[1])
            return v

        ld_gmin, ld_edges, ld_gbc = slot("ld_gmin"), slot("ld_edges"), slot("ld_gbc")
        grouped = acc[0:GP, 0, 0:GJ * GROUP * P].bitcast(I32)
        got_grouped = sp.dma(lambda e: e.dma_start(grouped, dst_grouped), ld_gmin)
        BA = 7
        stat6 = sb("stat6", [P, 2 * BA, 6])
        stat2 = sb("stat2", [P, 2 * BA, 2])
        std = sb("std", [P, 2 * BA])
        shift = sb("shift", [P, 2 * BA])
        pool.run(lambda e: e.memset(eps_sb[:, :], EPS))
        stats_zeroed = pool.run(lambda e: e.memset(stat2[:, :, :], 1.0))
        pool.run(lambda e: e.iota(iota_win[:, :], [[1, WIN]], base=0, channel_multiplier=0,
                                  allow_small_or_imprecise_dtypes=True))
        pool.run(lambda e: e.iota(iota_p[:, :], [[1, P]], base=0, channel_multiplier=0,
                                  allow_small_or_imprecise_dtypes=True))
        pool.run(lambda e: e.memset(ident[:, :], 0.0))
        pool.chain(lambda e: e.memset(ones[:, :], 1.0))
        pool.run(lambda e: e.affine_select(out=ident[:, :], in_=ident[:, :], compare_op=ALU.not_equal,
                                           fill=1.0, base=0, pattern=[[-1, P]], channel_multiplier=1))
        consts_ready = pool.run(lambda e: e.affine_select(
            out=upper[:, :], in_=ones[:, :], compare_op=ALU.is_ge, fill=0.0, base=0,
            pattern=[[1, P]], channel_multiplier=-1))

        gmin_cols = sb("gmin_cols", [P, GJ], I32)
        dve.wait(got_grouped)
        have_gmin = dve.run(lambda e: e.tensor_reduce(
            gmin_cols[0:GP, :], grouped.rearrange("p (j n) -> p j n", j=GJ), AX.X, ALU.min))

        pool.wait(have_gmin)
        acc_zeroed = pool.run(lambda e: e.memset(acc[:, :, :], 0.0))

        flag_f, flag_i = sb("flag_f", [P, 1]), sb("flag_i", [1, 1], I32)

        def edge_lists():
            dve.wait(got_edges, got_gmin)
            gm = gmin_sb[:, :].unsqueeze(2).broadcast_to([P, GROUPS, GROUP])
            dve.chain(lambda e: e.tensor_tensor(
                rel_sb[:, :].rearrange("p (g j) -> p g j", j=GROUP),
                rel_sb[:, :].bitcast(I32).rearrange("p (g j) -> p g j", j=GROUP), gm, ALU.subtract))
            far = rows_sb[:, :, :].rearrange("p a b -> p (a b)")[:, 0:CHUNKS]
            dve.chain(lambda e: e.scalar_tensor_tensor(far, rel_sb[:, :], float(WIN), wgt_sb[:, :],
                                                       ALU.is_ge, ALU.mult))
            dve.chain(lambda e: e.tensor_single_scalar(far, far, 0.0, ALU.not_equal))
            flagged = dve.chain(lambda e: e.tensor_reduce(flag_f[:, :], far, AX.X, ALU.max))
            pe.wait(flagged, consts_ready)
            spread = pe.run(lambda e: e.matmul(psum[0][0:1, 0:P], flag_f[:, :], ident[:, :],
                                               start=True, stop=True))
            dve.wait(spread)
            dve.chain(lambda e: e.tensor_reduce(flag_f[0:1, :], psum[0][0:1, 0:P], AX.X, ALU.max))
            return dve.chain(lambda e: e.tensor_copy(flag_i[:, :], flag_f[0:1, :]))

        A_SLOTS = 4
        xa = carve((A_SLOTS, BA, D), reset=0)
        x_ld = [slot(f"x_ld{i}") for i in range(A_SLOTS)]
        xn_st = [slot(f"xn_st{i}") for i in range(A_SLOTS)]
        batches = [range(b, min(b + BA, T)) for b in range(0, T, BA)]

        def batch_dmas(tiles, dram, view, width):
            full = [t for t in tiles if rows(t) == P]
            if full:
                d = dram[full[0] * P:(full[-1] + 1) * P, :].rearrange("(t p) d -> p t d", p=P)
                yield view[:, 0:len(full), :], d
            if len(full) < len(tiles):
                t, n = tiles[-1], rows(tiles[-1])
                yield view[0:n, len(full), :], dram[t * P:t * P + n, :]

        xn_stored = {}
        loaded_a = {}
        normed_a = {}
        on_dve = stats_zeroed
        ACT_TILES = 4

        def store_a(b):
            act.wait(*normed_a[b])
            s = b % A_SLOTS
            for frm, to in batch_dmas(batches[b], xn_d, xa[:, s], D):
                xn_stored[b] = act.dma(lambda e, to=to, frm=frm: e.dma_start(to, frm), xn_st[s])

        def load_a(b):
            s = b % A_SLOTS
            if b >= A_SLOTS:
                sp.wait(xn_stored[b - A_SLOTS])
            for to, frm in batch_dmas(batches[b], x, xa[:, s], D):
                loaded_a[b] = sp.dma(lambda e, to=to, frm=frm: e.dma_start(to, frm), x_ld[s])

        for b in range(min(3, len(batches))):
            load_a(b)
        for to, frm in ((rel_sb[:, :].bitcast(I32), dst), (wgt_sb[:, :], weight), (src_sb[:, :], src)):
            got_edges = sp.dma(lambda e, to=to, frm=frm: e.dma_start(to, frm), ld_edges)
        sp.wait(have_gmin)
        gmin_stored = sp.dma(lambda e: e.dma_start(gmin_d.rearrange("(p j) -> p j", j=GJ),
                                                   gmin_cols[0:GP, :]), ld_gmin)
        sp.wait(gmin_stored)
        got_gmin = sp.dma(lambda e: e.dma_start(
            gmin_sb[:, :], gmin_d.rearrange("(a g) -> a g", a=1).broadcast_to([P, GROUPS])), ld_gbc)
        for b, tiles in enumerate(batches):
            s, half = b % A_SLOTS, (b % 2) * BA
            n = len(tiles)
            dve.wait(loaded_a[b], stats_zeroed)
            if b >= 2:
                dve.wait(*normed_a[b - 2])
            for i, t in enumerate(tiles):
                r = rows(t)
                m = dve.run(lambda e, i=i, r=r, s=s, half=half: e.bn_stats(
                    stat6[0:r, half + i, :], xa[0:r, s, i, :]))
            dve.wait(m)
            for i, t in enumerate(tiles):
                r = rows(t)
                m = dve.run(lambda e, i=i, r=r, half=half: e.bn_aggr(
                    stat2[0:r, half + i, :], stat6[0:r, half + i, :]))
            act.wait(m)
            m = act.run(lambda e, half=half, n=n: e.activation(
                std[:, half:half + n], stat2[:, half:half + n, 1], ACT.Sqrt, bias=eps_sb[:, :]))
            dve.wait(m)
            dve.chain(lambda e, half=half, n=n: e.reciprocal(std[:, half:half + n], std[:, half:half + n]))
            nb = dve.run(lambda e, half=half, n=n: e.scalar_tensor_tensor(
                shift[:, half:half + n], stat2[:, half:half + n, 0], -1.0, std[:, half:half + n], ALU.mult, ALU.mult))
            act.wait(nb)
            for i, t in enumerate(tiles):
                r = rows(t)
                if i < ACT_TILES:
                    on_act = act.run(lambda e, i=i, r=r, s=s, half=half: e.activation(
                        xa[0:r, s, i, :], xa[0:r, s, i, :], ACT.Identity, bias=shift[0:r, half + i:half + i + 1],
                        scale=std[0:r, half + i:half + i + 1]))
                else:
                    on_dve = dve.run(lambda e, i=i, r=r, s=s, half=half: e.tensor_scalar(
                        xa[0:r, s, i, :], xa[0:r, s, i, :], stat2[0:r, half + i, 0:1],
                        std[0:r, half + i:half + i + 1], ALU.subtract, ALU.mult))
            if b >= 1:
                store_a(b - 1)
            normed_a[b] = (on_act, on_dve)
            if b + 3 < len(batches):
                load_a(b + 3)
        store_a(len(batches) - 1)
        flag_ready = edge_lists()
        all_xn_stored = [xn_stored[b] for b in range(max(0, len(batches) - A_SLOTS), len(batches))]

        taken[0] = 0
        R1 = 5
        xb = carve((R1, D))
        xnt = carve((R1, H, P))
        kvn = carve((2, 2 * D))
        sq = carve((2, 2 * D))
        top_b = taken[0]
        wkv_sb = carve((H, 2 * D))
        bkv_sb = carve((2 * D,))[0:1, :]
        gam_sb = carve((2 * D,))
        bet_sb = carve((2 * D,))
        wsum = sb("wsum", [P, H, 2 * HEADS])
        weff = sb("weff", [P, H, D])
        beff = sb("beff", [P, H])
        w1m_sb = carve((H, D))
        wqt_sb = carve((H, D + 1))
        pt_sb = carve((H, D + 1))
        w2m_sb = sb("w2m_sb", [P, H, D])
        w1g_sb = sb("w1g_sb", [P, H, D])
        w2g_sb = sb("w2g_sb", [P, H, D])
        b2m_sb = sb("b2m_sb", [1, D])
        bg_sb = sb("bg_sb", [1, 2, D])
        b1m_sb = sb("b1m_sb", [P, H])
        kv_bd = carve((H, P))
        ss = sb("ss", [P, 2, 2 * HEADS])
        gate_sb = sb("gate_sb", [P, H, NE])
        gateb_sb = sb("gateb_sb", [P, NE])

        def halves(w):
            return w.rearrange("(h p) f -> p h f", p=P)

        def row(v):
            return v.rearrange("(a d) -> a d", a=1)

        def everywhere(v, n):
            return row(v).broadcast_to([P, n])

        wld, wld2 = slot("weights_ld"), slot("weights_ld_late")
        sp.wait(*all_xn_stored)
        early = [(wkv_sb[:, :, :], halves(wkv)), (bkv_sb[:, :], row(bkv)),
                 (gam_sb, everywhere(kv_gamma, 2 * D)), (bet_sb, everywhere(kv_beta, 2 * D))]
        late = [(w1m_sb, halves(mix_w1)), (wqt_sb, halves(wqt_bq)), (w2m_sb[:, :, :], halves(mix_w2)),
                (w1g_sb[:, :, :], halves(gnn_w1t)), (w2g_sb[:, :, :], halves(gnn_w2t)),
                (b2m_sb[:, :], row(mix_b2)), (bg_sb[:, 0, :], row(gnn_b1)), (bg_sb[:, 1, :], row(gnn_b2)),
                (b1m_sb[:, :], mix_b1), (gate_sb[:, :, :], halves(gate_w)),
                (gateb_sb[:, :], everywhere(gate_b, NE))]
        for to, frm in early:
            got_early = sp.dma(lambda e, to=to, frm=frm: e.dma_start(to, frm), wld)
        for to, frm in late:
            got_late = sp.dma(lambda e, to=to, frm=frm: e.dma_start(to, frm), wld2)

        def centre(w, sums):
            dve.chain(lambda e: e.tensor_reduce(sums, w.rearrange("p (h c) -> p h c", c=HEADC), AX.X, ALU.add))
            dve.chain(lambda e: e.tensor_single_scalar(sums, sums, 1.0 / HEADC, ALU.mult))
            return dve.chain(lambda e: e.tensor_tensor(
                w.rearrange("p (h c) -> p h c", c=HEADC), w.rearrange("p (h c) -> p h c", c=HEADC),
                sums.unsqueeze(2).broadcast_to([w.shape[0], 2 * HEADS, HEADC]), ALU.subtract))

        def centre_all():
            dve.wait(got_early)
            for h in range(H):
                centre(wkv_sb[:, h, :], wsum[:, h, :])
            return centre(bkv_sb[:, :], wsum[0:1, 0, :])

        row_ld = [slot(f"row_ld{i}") for i in range(ROW_SLOTS)]
        s_ready, group_mm, group_added, group_copied, group_turned = {}, {}, {}, {}, {}
        SUM_SLOTS = 3
        sums = sb("sums", [WIN, SUM_SLOTS, D])

        def build_s(k):
            g0, n = S_GROUPS * k, min(S_GROUPS, GROUPS - S_GROUPS * k)
            last_reader = g0 - S_GROUPS * (S_SLOTS - 1) - 1
            if k >= S_SLOTS:
                dve.wait(group_mm[last_reader])
            c0, c = g0 * GROUP, n * GROUP
            s = s_sb[:, k % S_SLOTS, 0:c, :]
            wide = [P, c, WIN]
            dve.chain(lambda e: e.tensor_tensor(
                s, rel_sb[:, c0:c0 + c].unsqueeze(2).broadcast_to(wide),
                iota_win[:, :].unsqueeze(1).broadcast_to(wide), ALU.is_equal))
            m = dve.run(lambda e: e.tensor_tensor(
                s, s, wgt_sb[:, c0:c0 + c].unsqueeze(2).broadcast_to(wide), ALU.mult))
            for g in range(g0, g0 + n):
                s_ready[g] = m

        def gather_group(g):
            for c in range(g * GROUP, (g + 1) * GROUP):
                if g >= ROW_SLOTS // GROUP:
                    pool.wait(group_mm[g - ROW_SLOTS // GROUP])
                pool.dma(lambda e, c=c: e.indirect_dma_start(
                    out=rows_sb[:, c % ROW_SLOTS, :], out_offset=None, in_=xn_d,
                    in_offset=bass.IndirectOffsetOnAxis(ap=src_sb[:, c:c + 1], axis=0)),
                    row_ld[c % ROW_SLOTS])

        def multiply_group(g):
            pe.wait(s_ready[g])
            for j in range(GROUP):
                c = g * GROUP + j
                pe.wait((row_ld[c % ROW_SLOTS][0], 16 * (c // ROW_SLOTS + 1)))
            if g >= 2:
                pe.wait(group_copied[g - 2])
            k, j0 = g // S_GROUPS, (g % S_GROUPS) * GROUP
            for j in range(GROUP):
                c = g * GROUP + j
                m = pe.run(lambda e, j=j, c=c: e.matmul(
                    psum[g % 2][0:WIN, 0:D], s_sb[:, k % S_SLOTS, j0 + j, :], rows_sb[:, c % ROW_SLOTS, :],
                    start=j == 0, stop=j == GROUP - 1), tell=j == GROUP - 1)
            group_mm[g] = m
            act.wait(m)
            if g >= SUM_SLOTS:
                act.wait(group_turned[g - SUM_SLOTS])
            group_copied[g] = act.run(lambda e: e.copy(sums[0:WIN, g % SUM_SLOTS, :], psum[g % 2][0:WIN, 0:D]))

        def turn_group(g):
            pe.wait(group_copied[g])
            if g:
                pe.wait(group_added[g - 1])
            for h in range(H):
                m = pe.run(lambda e, h=h: e.transpose(
                    psum[7][:, h * WIN:(h + 1) * WIN], sums[0:WIN, g % SUM_SLOTS, h * P:(h + 1) * P],
                    ident[0:WIN, 0:WIN]), tell=h == H - 1)
            group_turned[g] = m

        def add_group(g):
            dve.wait(group_turned[g])

            def step(e):
                at = e.value_load(gmin_sb[0:1, g:g + 1], min_val=0, max_val=N - 1)
                win = acc[:, :, bass.ds(at, WIN)]
                return e.tensor_tensor(win, win, psum[7][:, 0:H * WIN].rearrange(
                    "p (h w) -> p h w", h=H), ALU.add)
            group_added[g] = dve.chain(step)

        xn_ld = [slot(f"xn_ld{i}") for i in range(R1)]
        xnt_st = [slot(f"xnt_st{i}") for i in range(R1)]
        xb_free, xnt_stored, kv_read, kvn_read, sq_read, tr_read = {}, {}, {}, {}, {}, {}
        state = {}

        def node_kv(t):
            r, s, par = rows(t), t % R1, t % 2
            if t >= R1:
                sp.wait(xb_free[t - R1])
            loaded = sp.dma(lambda e: e.dma_start(xb[0:r, s, :], xn_d[t * P:t * P + r, :]), xn_ld[s])
            yield
            pe.wait(loaded, consts_ready)
            if t >= 1:
                pe.wait(tr_read[t - 1])
            for h in range(H):
                m = pe.run(lambda e, h=h: e.transpose(psum[4][:, h * P:h * P + r],
                                                      xb[0:r, s, h * P:(h + 1) * P], ident[0:r, 0:r]),
                           tell=h == H - 1)
            xb_free[t] = m
            act.wait(m)
            if t >= R1:
                act.wait(xnt_stored[t - R1])
                act.wait(kv_read[t - R1])
            tr_read[t] = act.run(lambda e: e.copy(
                xnt[:, s, :, 0:r], psum[4][:, 0:H * P].rearrange("p (h n) -> p h n", h=H)[:, :, 0:r]))
            yield
            sp.wait(tr_read[t])
            xnt_stored[t] = sp.dma(lambda e: e.dma_start(
                xnt_d[:, :, t * P:t * P + r].rearrange("h p n -> p h n"), xnt[:, s, :, 0:r]), xnt_st[s])
            pe.wait(state["centred"], tr_read[t])
            if t >= 2:
                pe.wait(kvn_read[t - 2, "psum"])
            kv = psum[2 + par]
            pe.run(lambda e: e.matmul(kv[0:r, :], ones[0:1, 0:r], bkv_sb[:, :], start=True, stop=False), tell=False)
            for h in range(H):
                m = pe.run(lambda e, h=h: e.matmul(kv[0:r, :], xnt[:, s, h, 0:r], wkv_sb[:, h, :],
                                                   start=False, stop=h == H - 1), tell=h == H - 1)
            kv_read[t] = m
            act.wait(m)
            if t >= 2:
                act.wait(sq_read[t - 2])
            squared = act.run(lambda e: e.activation(sq[0:r, par, :], kv[0:r, :], ACT.Square))
            yield
            dve.wait(squared)
            sq_read[t] = dve.run(lambda e: e.tensor_reduce(
                ss[0:r, par, :], sq[0:r, par, :].rearrange("p (h c) -> p h c", c=HEADC), AX.X, ALU.add))
            act.wait(sq_read[t])
            rooted = act.run(lambda e: e.activation(ss[0:r, par, :], ss[0:r, par, :], ACT.Sqrt,
                                                    bias=eps_sb[0:r, :], scale=1.0 / HEADC))
            yield
            dve.wait(rooted)
            dve.chain(lambda e: e.reciprocal(ss[0:r, par, :], ss[0:r, par, :]))
            if t >= 2:
                dve.wait(kvn_read[t - 2])
            kvn_read[t, "psum"] = dve.chain(lambda e: e.tensor_tensor(
                kvn[0:r, par, :].rearrange("p (h c) -> p h c", c=HEADC),
                kv[0:r, :].rearrange("p (h c) -> p h c", c=HEADC),
                ss[0:r, par, :].unsqueeze(2).broadcast_to([r, 2 * HEADS, HEADC]), ALU.mult))
            dve.chain(lambda e: e.tensor_tensor(kvn[0:r, par, :], kvn[0:r, par, :], gam_sb[0:r, :], ALU.mult))
            m = dve.run(lambda e: e.tensor_tensor(kvn[0:r, par, :], kvn[0:r, par, :], bet_sb[0:r, :], ALU.add))
            yield
            pe.wait(m)
            for h in range(H):
                m = pe.run(lambda e, h=h: e.matmul(
                    psum[5 + h][:, 0:P], kvn[0:r, par, h * P:(h + 1) * P],
                    kvn[0:r, par, D + h * P:D + (h + 1) * P], start=t == 0, stop=t == T - 1),
                    tell=h == H - 1)
            kvn_read[t] = m

        def fold():
            z = dve.chain(lambda e: e.memset(kv_bd, 0.0))
            dve.wait(kvn_read[T - 1])
            for h in range(H):
                for q in range(P // HEADC):
                    a, b = q * HEADC, (q + 1) * HEADC
                    m = dve.run(lambda e, h=h, a=a, b=b: e.tensor_single_scalar(
                        kv_bd[a:b, h, a:b], psum[5 + h][a:b, a:b], 1.0 / N, ALU.mult))
            yield
            pe.wait(m, got_late)
            for h in range(H):
                m = pe.run(lambda e, h=h: e.matmul(psum[2 + h][:, 0:D + 1], kv_bd[:, h, :], wqt_sb[:, h, :],
                                                   start=True, stop=True))
            dve.wait(m)
            for h in range(H):
                dve.chain(lambda e, h=h: e.tensor_copy(pt_sb[:, h, :], psum[2 + h][:, 0:D + 1]))
                m = dve.chain(lambda e, h=h: e.tensor_tensor(pt_sb[:, h, h * P:(h + 1) * P],
                                                             pt_sb[:, h, h * P:(h + 1) * P], ident[:, :], ALU.add))
            m2 = dve.chain(lambda e: e.tensor_tensor(bg_sb[:, 0, :], bg_sb[:, 0, :], bg_sb[:, 1, :], ALU.add))
            yield
            pe.wait(m, m2)
            for i in range(H):
                for h in range(H):
                    pe.run(lambda e, i=i, h=h: e.matmul(psum[4 + i][:, 0:D], pt_sb[:, h, i * P:(i + 1) * P],
                                                        w1m_sb[:, h, :], start=h == 0, stop=h == H - 1), tell=False)
            for i in range(H):
                for h in range(H):
                    m = pe.run(lambda e, i=i, h=h: e.matmul(
                        psum[2 + i][:, 0:1], w1m_sb[:, h, i * P:(i + 1) * P], pt_sb[:, h, D:D + 1],
                        start=h == 0, stop=h == H - 1))
            dve.wait(m)
            for i in range(H):
                dve.run(lambda e, i=i: e.tensor_copy(weff[:, i, :], psum[4 + i][:, 0:D]))
                m = dve.run(lambda e, i=i: e.tensor_tensor(beff[:, i:i + 1], psum[2 + i][:, 0:1],
                                                           b1m_sb[:, i:i + 1], ALU.add))
            state["folded"] = m
            yield

        Q = 4
        UNITS = -(-T // Q)
        save = taken[0]
        taken[0] = 0
        xq = carve((2, H, Q * P))
        hq = carve((2, H, Q * P))
        RO = 4
        xr = carve((RO, 2, D))
        ego_o = carve((RO, D))
        base_o = carve((RO, D))
        top_b2 = taken[0]
        xq_ld = [slot(f"xq_ld{i}") for i in range(2)]
        xr_ld = [slot(f"xr_ld{i}") for i in range(RO)]
        out_st = [slot(f"be_st{i}") for i in range(RO)]
        xq_read, hq_read, ht_read, mix_read, be_stored, base_made = {}, {}, {}, {}, {}, {}

        have_rows = {}

        def load_rows(t):
            r, o = rows(t), t % RO
            if t >= RO:
                sp.wait(base_made[t - RO])
            sp.dma(lambda e: e.dma_start(xr[0:r, o, 0, :], x[t * P:t * P + r, :]), xr_ld[o])
            have_rows[t] = sp.dma(lambda e: e.dma_start(xr[0:r, o, 1, :], xn_d[t * P:t * P + r, :]), xr_ld[o])

        def node_mix(u):
            tiles = range(u * Q, min(u * Q + Q, T))
            n = sum(rows(t) for t in tiles)
            s = u % 2
            if u == 0:
                sp.wait(state["folded"], *[xnt_stored[t] for t in range(max(0, T - R1), T)])
                load_rows(0)
            if u >= 2:
                sp.wait(xq_read[u - 2])
            loaded = sp.dma(lambda e: e.dma_start(
                xq[:, s, :, 0:n], xnt_d[:, :, u * Q * P:u * Q * P + n].rearrange("h p n -> p h n")), xq_ld[s])
            yield
            pe.wait(loaded, state["folded"])
            if u >= 2:
                act.wait(hq_read[u - 2])
            for f in range(H):
                if (u, f) != (0, f):
                    pe.wait(ht_read[u - 1, f])
                for h in range(H):
                    m = pe.run(lambda e, f=f, h=h: e.matmul(
                        psum[2 + f][:, 0:n], weff[:, h, f * P:(f + 1) * P], xq[:, s, h, 0:n],
                        start=h == 0, stop=h == H - 1), tell=h == H - 1)
                act.wait(m)
                ht_read[u, f] = act.run(lambda e, f=f: e.activation(
                    hq[:, s, f, 0:n], psum[2 + f][:, 0:n], ACT.Gelu, bias=beff[:, f:f + 1]))
                yield
            for t in tiles:
                r, i, o, bank = rows(t), t - u * Q, t % RO, 4 + t % 2
                if t + 1 < T:
                    load_rows(t + 1)
                have = have_rows[t]
                pe.wait(ht_read[u, H - 1])
                if t >= 2:
                    pe.wait(*mix_read[t - 2])
                mix, ego = psum[bank][0:r, 0:D], psum[bank][0:r, D:2 * D]
                pe.run(lambda e, r=r, mix=mix: e.matmul(mix, ones[0:1, 0:r], b2m_sb[:, :], start=True, stop=False), tell=False)
                for f in range(H):
                    pe.run(lambda e, f=f, r=r, i=i, mix=mix: e.matmul(
                        mix, hq[:, s, f, i * P:i * P + r], w2m_sb[:, f, :], start=False, stop=f == H - 1), tell=False)
                pe.run(lambda e, r=r, ego=ego: e.matmul(ego, ones[0:1, 0:r], bg_sb[:, 0, :], start=True, stop=False), tell=False)
                for h in range(H):
                    m = pe.run(lambda e, h=h, r=r, i=i, ego=ego: e.matmul(
                        ego, xq[:, s, h, i * P:i * P + r], w1g_sb[:, h, :], start=False, stop=h == H - 1),
                        tell=h == H - 1)
                act.wait(m)
                if t >= RO:
                    act.wait(be_stored[t - RO])
                    dve.wait(be_stored[t - RO])
                a = act.run(lambda e, r=r, o=o, ego=ego: e.copy(ego_o[0:r, o, :], ego))
                dve.wait(m, have, a)
                d = dve.chain(lambda e, r=r, o=o, mix=mix: e.tensor_tensor(
                    base_o[0:r, o, :], mix, xr[0:r, o, 1, :], ALU.add))
                mix_read[t] = (a, d)
                d2 = dve.run(lambda e, r=r, o=o: e.tensor_tensor(
                    base_o[0:r, o, :], base_o[0:r, o, :], xr[0:r, o, 0, :], ALU.add))
                base_made[t] = d2
                act.wait(d2)
                act.dma(lambda e, t=t, r=r, o=o: e.dma_start(ego_d[t * P:t * P + r, :], ego_o[0:r, o, :]), out_st[o])
                be_stored[t] = act.dma(lambda e, t=t, r=r, o=o: e.dma_start(
                    base_d[t * P:t * P + r, :], base_o[0:r, o, :]), out_st[o])
                yield
            xq_read[u] = m
            hq_read[u] = m

        taken[0] = save

        def nodes_of_b():
            yield from run_skewed(node_kv(t) for t in range(T))
            yield from fold()
            unit = node_mix(0)
            next(unit)
            for u in range(UNITS):
                ahead = node_mix(u + 1) if u + 1 < UNITS else None
                for piece, _ in enumerate(unit):
                    if piece == H + 1 and ahead:
                        next(ahead)
                        yield
                        continue
                    yield
                unit = ahead

        state["centred"] = centre_all()
        pool.wait(*all_xn_stored, acc_zeroed, got_edges, flag_ready)
        dve.wait(acc_zeroed)
        total = T + 5 + 3 + UNITS * H + T
        side = nodes_of_b()
        done_ticks = 0
        build_s(0)
        for g in range(GROUPS):
            gather_group(g)
            if g % S_GROUPS == 0 and g + S_GROUPS < GROUPS:
                build_s(g // S_GROUPS + 1)
            multiply_group(g)
            if g > 1:
                add_group(g - 2)
            if g:
                turn_group(g - 1)
            while done_ticks * (GROUPS - 4) < total * (g + 1):
                next(side, None)
                done_ticks += 1
        if GROUPS > 1:
            add_group(GROUPS - 2)
        turn_group(GROUPS - 1)
        add_group(GROUPS - 1)
        for _ in side:
            pass

        far_rows, far_s, far_sum, far_done = sem("far_rows"), sem("far_s"), sem("far_sum"), sem("far_done")
        far_dve, far_pool = sem("far_dve"), sem("far_pool")
        WIDE_SLOTS = 2
        far_idx = sb("far_idx", [P, 1], I32)
        far_w = sb("far_w", [P, 1])
        far_at = sb("far_at", [P, WIDE_WINDOWS])
        far_steps = sb("far_steps", [P, WIDE_WINDOWS])
        iota_wide = carve((WIDE,), reset=top_b2)
        s_wide = carve((WIDE_SLOTS, WIDE))
        row_buf = rows_sb[:, 0, :]
        groups_over = (group_mm[GROUPS - 1], group_added[GROUPS - 1])

        def far_pool_lane(e):
            flag = e.value_load(flag_i[:, :], min_val=0, max_val=1)
            with e.If(flag):
                e.iota(iota_wide, [[1, WIDE]], base=0, channel_multiplier=0,
                       allow_small_or_imprecise_dtypes=True).then_inc(far_pool, 1)
                e.iota(far_steps[:, :], [[-WIDE, WIDE_WINDOWS]], base=0, channel_multiplier=0,
                       allow_small_or_imprecise_dtypes=True).then_inc(far_pool, 1)
                with nc.Fori(0, CHUNKS, engines=[mybir.EngineType.Pool]) as c:
                    e.tensor_copy(far_idx[:, :], src_sb[:, bass.ds(c, 1)]).then_inc(far_done, 1)
                    e.wait_ge(far_done, 1)
                    e.sem_clear(far_done)
                    e.indirect_dma_start(out=row_buf, out_offset=None, in_=xn_d,
                                         in_offset=bass.IndirectOffsetOnAxis(ap=far_idx[:, :], axis=0)
                                         ).then_inc(far_rows, 16)
                    e.wait_ge(far_done, 1)
                    e.sem_clear(far_done)

        def far_pe_lane(e):
            flag = e.value_load(flag_i[:, :], min_val=0, max_val=1)
            with e.If(flag):
                with nc.Fori(0, CHUNKS, engines=[mybir.EngineType.PE]) as c:
                    e.wait_ge(far_rows, (c + 1) * 16)
                    for u in range(WIDE_WINDOWS):
                        e.wait_ge(far_s, u + 1)
                        if u == WIDE_WINDOWS - 1:
                            e.sem_clear(far_s)
                        for h in range(H):
                            m = e.matmul(psum[h][:, 0:WIDE], rows_sb[:, 0, h * P:(h + 1) * P],
                                         s_wide[:, u % WIDE_SLOTS, :], start=True, stop=True)
                        m.then_inc(far_sum, 1)

        def far_dve_lane(e):
            flag = e.value_load(flag_i[:, :], min_val=0, max_val=1)
            with e.If(flag):
                e.wait_ge(far_pool, 2)
                with nc.Fori(0, CHUNKS, engines=[mybir.EngineType.DVE]) as c:
                    step = [0]

                    def link(ins):
                        step[0] += 1
                        ins.then_inc(far_dve, 1)
                        e.wait_ge(far_dve, step[0])
                    link(e.scalar_tensor_tensor(far_w[:, :], rel_sb[:, bass.ds(c, 1)], float(WIN),
                                                wgt_sb[:, bass.ds(c, 1)], ALU.is_ge, ALU.mult))
                    link(e.tensor_tensor(far_at[:, 0:1], rel_sb[:, bass.ds(c, 1)], gmin_sb[:, bass.ds(c // GROUP, 1)], ALU.add))
                    link(e.tensor_scalar(far_at[:, 1:], far_steps[:, 1:], far_at[:, 0:1], None, ALU.add)
                         if WIDE_WINDOWS > 1 else e.tensor_copy(far_at[:, 0:1], far_at[:, 0:1]))
                    for u in range(WIDE_WINDOWS):
                        link(e.tensor_scalar(s_wide[:, u % WIDE_SLOTS, :], iota_wide, far_at[:, u:u + 1],
                                             far_w[:, :], ALU.is_equal, ALU.mult))
                        e.sem_inc(far_s, 1)
                        e.wait_ge(far_sum, u + 1)
                        for h in range(H):
                            win = acc[:, h, u * WIDE:(u + 1) * WIDE]
                            link(e.tensor_tensor(win, win, psum[h][:, 0:WIDE], ALU.add))
                    e.sem_clear(far_sum)
                    e.sem_clear(far_dve)
                    e.sem_inc(far_done, 1)

        for lane in (pool, pe, dve):
            lane.wait(flag_ready, *groups_over, *mix_read[T - 1])
        pool.run(far_pool_lane, tell=False)
        pe.run(far_pe_lane, tell=False)
        dve.run(far_dve_lane, tell=False)

        BC = 2
        C_UNITS = -(-T // BC)
        RC, RW = 4, 5
        taken[0] = 0
        xc = carve((RC, H, BC * P))
        ec = carve((RW, BC * D))
        bc = carve((RW, BC * D))
        comb = carve((RC, BC * 2 * D))
        junk = s_sb[:, :, :, :].rearrange("p a b w -> p (a b w)")[:, 0:BC * D]
        h2t = carve((2, BC * H * P))
        nrm = sb("nrm", [P, RW, BC])
        c_ld = [slot(f"c_ld{i}") for i in range(RW)]
        c_st = [slot(f"c_st{i}") for i in range(RC)]
        mt_read, side_read, comb_stored, trc_read, logit_mm, base_used = {}, {}, {}, {}, {}, {}
        TH = -(-T // 2)
        b_over = [be_stored[t] for t in range(max(0, T - RO), T)]

        def node_out(u):
            tiles = range(u * BC, min(u * BC + BC, T))
            nt, s, w, par = len(tiles), u % RC, u % RW, u % 2
            n = sum(rows(t) for t in tiles)
            whole = all(rows(t) == P for t in tiles)
            if u == 0:
                sp.wait(*b_over, group_mm[max(0, GROUPS - 3)])
            if u >= RC:
                sp.wait(mt_read[u - RC])
            if u >= RW:
                sp.wait(*base_used[u - RW])
            sp.dma(lambda e: e.dma_start(
                xc[:, s, :, 0:n], xnt_d[:, :, u * BC * P:u * BC * P + n].rearrange("h p n -> p h n")), c_ld[w])
            for dram, buf in ((ego_d, ec), (base_d, bc)):
                view = buf[:, w, :].rearrange("p (t d) -> p t d", d=D)
                for to, frm in batch_dmas(list(tiles), dram, view, D):
                    loaded = sp.dma(lambda e, to=to, frm=frm: e.dma_start(to, frm), c_ld[w])
            yield
            pool.wait(loaded)
            sums_t = acc[:, :, u * BC * P:u * BC * P + n]
            pool.chain(lambda e: e.tensor_tensor(xc[:, s, :, 0:n], xc[:, s, :, 0:n], sums_t, ALU.mult))
            summed = pool.run(lambda e: e.tensor_tensor(xc[:, s, :, 0:n], xc[:, s, :, 0:n], sums_t, ALU.add))
            state["acc_free"] = summed
            yield
            pe.wait(summed)
            if u >= 2:
                pe.wait(side_read[u - 2])
            for i, t in enumerate(tiles):
                r = rows(t)
                for h in range(H):
                    m = pe.run(lambda e, i=i, h=h, r=r: e.matmul(
                        psum[par][0:r, i * D:(i + 1) * D], xc[:, s, h, i * P:i * P + r], w2g_sb[:, h, :],
                        start=h == 0, stop=h == H - 1), tell=h == H - 1)
            mt_read[u] = m
            yield
            dve.wait(m)

            def pieces(view, width):
                if whole:
                    return [view[:, 0:nt * width]]
                return [view[0:rows(t), i * width:(i + 1) * width] for i, t in enumerate(tiles)]

            for o, ps in zip(pieces(ec[:, w, :], D), pieces(psum[par], D)):
                m = dve.run(lambda e, o=o, ps=ps: e.tensor_tensor(o, o, ps, ALU.add))
            side_read[u] = m
            dve.wait(m)
            for o in pieces(ec[:, w, :], D):
                m = dve.run(lambda e, o=o: e.scalar_tensor_tensor(o, o, LEAKY, o, ALU.mult, ALU.max))
            act.wait(m)
            for i, t in enumerate(tiles):
                r = rows(t)
                a = act.chain(lambda e, i=i, r=r: e.activation(
                    junk[0:r, i * D:(i + 1) * D], ec[0:r, w, i * D:(i + 1) * D], ACT.Square,
                    accum_out=nrm[0:r, w, i:i + 1]))
            for i, t in enumerate(tiles) if not whole else [(0, None)]:
                v = nrm[:, w, 0:nt] if whole else nrm[0:rows(t), w, i:i + 1]
                a = act.run(lambda e, v=v: e.activation(v, v, ACT.Sqrt))
            yield
            dve.wait(a)
            for i, t in enumerate(tiles) if not whole else [(0, None)]:
                v = nrm[:, w, 0:nt] if whole else nrm[0:rows(t), w, i:i + 1]
                dve.chain(lambda e, v=v: e.tensor_single_scalar(v, v, NORM_EPS, ALU.max))
                scale_ready = dve.run(lambda e, v=v: e.reciprocal(v, v))
            cview = comb[:, s, :].rearrange("p (t w d) -> p t w d", w=2, d=D)
            act.wait(scale_ready)
            dve.wait(scale_ready)
            if u >= RC:
                pool.wait(comb_stored[u - RC])
                dve.wait(comb_stored[u - RC])
            made = []
            for i, t in enumerate(tiles):
                r = rows(t)
                gnn, base = (b[0:r, w, i * D:(i + 1) * D] for b in (ec, bc))
                if i % 2:
                    made.append(dve.run(lambda e, i=i, r=r, gnn=gnn, base=base: e.scalar_tensor_tensor(
                        cview[0:r, i, 1, :], gnn, nrm[0:r, w, i:i + 1], base, ALU.mult, ALU.add)))
                    continue
                a = act.run(lambda e, i=i, r=r, gnn=gnn: e.activation(gnn, gnn, ACT.Copy, scale=nrm[0:r, w, i:i + 1]))
                pool.wait(a)
                made.append(pool.run(lambda e, i=i, r=r, gnn=gnn, base=base: e.tensor_tensor(
                    cview[0:r, i, 1, :], gnn, base, ALU.add)))
            base_used[u] = made
            yield
            dve.wait(*made)
            for i, t in enumerate(tiles):
                r = rows(t)
                m = dve.run(lambda e, i=i, r=r: e.bn_stats(stat6[0:r, par * BC + i, :], cview[0:r, i, 1, :]))
            dve.wait(m)
            for i, t in enumerate(tiles):
                r = rows(t)
                m = dve.run(lambda e, i=i, r=r: e.bn_aggr(stat2[0:r, par * BC + i, :], stat6[0:r, par * BC + i, :]))
            act.wait(m)
            a = act.run(lambda e: e.activation(std[:, par * BC:par * BC + nt],
                                               stat2[:, par * BC:par * BC + nt, 1], ACT.Sqrt, bias=eps_sb[:, :]))
            yield
            dve.wait(a)
            dve.chain(lambda e: e.reciprocal(std[:, par * BC:par * BC + nt], std[:, par * BC:par * BC + nt]))
            for i, t in enumerate(tiles):
                r = rows(t)
                m = dve.run(lambda e, i=i, r=r: e.tensor_scalar(
                    cview[0:r, i, 0, :], cview[0:r, i, 1, :], stat2[0:r, par * BC + i, 0:1],
                    std[0:r, par * BC + i:par * BC + i + 1], ALU.subtract, ALU.mult))
            normed = m
            act.wait(m)
            for i, t in enumerate(tiles):
                r = rows(t)
                act.dma(lambda e, i=i, t=t, r=r: e.dma_start(
                    h2_d[t * P:t * P + r, :], cview[0:r, i, 0, :]), c_st[s])
                comb_stored[u] = act.dma(lambda e, i=i, t=t, r=r: e.dma_start(
                    out[t * P:t * P + r, :], cview[0:r, i, 1, :]), c_st[s])
            pe.wait(normed)
            if u >= 2:
                pe.wait(trc_read[u - 2])
            for i, t in enumerate(tiles):
                r = rows(t)
                for h in range(H):
                    m = pe.run(lambda e, i=i, h=h, r=r: e.transpose(
                        psum[2 + par][:, (i * H + h) * P:(i * H + h) * P + r], cview[0:r, i, 0, h * P:(h + 1) * P],
                        ident[0:r, 0:r]), tell=h == H - 1)
            act.wait(m)
            if u >= 2:
                act.wait(logit_mm[u - 2])
            for i, t in enumerate(tiles):
                r = rows(t)
                a = act.run(lambda e, i=i, r=r: e.copy(
                    h2t[:, par, i * D:(i + 1) * D].rearrange("p (h n) -> p h n", h=H)[:, :, 0:r],
                    psum[2 + par][:, i * D:(i + 1) * D].rearrange("p (h n) -> p h n", h=H)[:, :, 0:r]))
            trc_read[u] = a
            yield
            pe.wait(a)
            for i, t in enumerate(tiles):
                r = rows(t)
                lg = psum[6 + t // TH][0:r, (t % TH) * NE:(t % TH + 1) * NE]
                for h in range(H):
                    m = pe.run(lambda e, i=i, h=h, r=r, lg=lg: e.matmul(
                        lg, h2t[:, par, (i * H + h) * P:(i * H + h) * P + r], gate_sb[:, h, :],
                        start=h == 0, stop=h == H - 1), tell=h == H - 1)
            logit_mm[u] = m

        for _ in run_skewed((node_out(u) for u in range(C_UNITS)), youngest_first=True):
            pass
        c_stored = [comb_stored[u] for u in range(max(0, C_UNITS - RC), C_UNITS)]

        flat = acc[:, :, :].rearrange("p h w -> p (h w)")
        behind = [0]

        def route_buf(*shape):
            at, n = behind[0], math.prod(shape)
            behind[0] += n
            v = flat[:, at:at + n]
            return v if len(shape) == 1 else v.rearrange("p (a b) -> p a b", a=shape[0])
        lg, hot, tmp, tot = (route_buf(T, NE) for _ in range(4))
        c1 = route_buf(T)
        prb = route_buf(T)
        lo = route_buf(T)
        hi = route_buf(T)
        ids = route_buf(T)
        pos_i = route_buf(T).bitcast(I32)
        e_desc = sb("e_desc", [P, NE])
        e_base = sb("e_base", [P, NE])
        rl = rows(T - 1)

        def tall(v):
            return v.unsqueeze(2).broadcast_to([P, T, NE])

        def per_expert(v):
            return v.unsqueeze(1).broadcast_to([P, T, NE])

        pool.wait(state["acc_free"])
        dve.wait(state["acc_free"])
        pool.run(lambda e: e.iota(e_desc[:, :], [[-1, NE]], base=NE, channel_multiplier=0,
                                  allow_small_or_imprecise_dtypes=True))
        pool.run(lambda e: e.iota(e_base[:, :], [[SLOT_TILES, NE]], base=0, channel_multiplier=0,
                                  allow_small_or_imprecise_dtypes=True))
        ids_ready = pool.run(lambda e: e.iota(ids[:, :], [[P, T]], base=1, channel_multiplier=1,
                                              allow_small_or_imprecise_dtypes=True))
        dve.chain(lambda e: e.memset(lg[:, T - 1, :], 0.0))
        dve.wait(logit_mm[C_UNITS - 1], ids_ready)

        def logits_plus_bias(t0, t1, r):
            bank = psum[6 + t0 // TH][0:r, (t0 % TH) * NE:(t0 % TH + t1 - t0) * NE].rearrange(
                "p (t e) -> p t e", e=NE)
            return dve.run(lambda e: e.tensor_tensor(
                lg[0:r, t0:t1, :], bank, gateb_sb[0:r, :].unsqueeze(1).broadcast_to([r, t1 - t0, NE]), ALU.add))
        spans = [(0, min(TH, T - 1), P), (TH, T - 1, P), (T - 1, T, rl)]
        for t0, t1, r in spans:
            if t1 > t0:
                m = logits_plus_bias(t0, t1, r)
        dve.wait(m)
        dve.chain(lambda e: e.tensor_reduce(c1[:, :], lg, AX.X, ALU.max))
        m_shift = dve.chain(lambda e: e.tensor_tensor(lg, lg, tall(c1[:, :]), ALU.subtract))
        act.wait(m_shift)
        a = act.run(lambda e: e.activation(tmp, lg, ACT.Exp))
        dve.chain(lambda e: e.tensor_single_scalar(hot, lg, 0.0, ALU.is_equal))
        dve.chain(lambda e: e.tensor_tensor(hot, hot, per_expert(e_desc[:, :]), ALU.mult))
        dve.chain(lambda e: e.tensor_reduce(c1[:, :], hot, AX.X, ALU.max))
        dve.chain(lambda e: e.tensor_tensor(hot, hot, tall(c1[:, :]), ALU.is_equal))
        if rl < P:
            dve.chain(lambda e: e.tensor_copy(tot[:, T - 1, :], hot[:, T - 1, :]))
            dve.chain(lambda e: e.memset(hot[:, T - 1, :], 0.0))
            dve.chain(lambda e: e.tensor_copy(hot[0:rl, T - 1, :], tot[0:rl, T - 1, :]))
        hot_ready = dve.chain(lambda e: e.tensor_reduce(c1[:, :], hot, AX.X, ALU.max))
        dve.wait(a)
        dve.chain(lambda e: e.tensor_reduce(prb[:, :], tmp, AX.X, ALU.add))
        dve.chain(lambda e: e.reciprocal(prb[:, :], prb[:, :]))
        pe.wait(hot_ready)
        cuts = [(0, TH), (TH, T)]
        for k, (t0, t1) in enumerate(cuts):
            hv = hot[:, t0:t1, :].rearrange("p t e -> p (t e)")
            pe.run(lambda e, k=k, hv=hv: e.matmul(psum[k][:, 0:hv.shape[1]], upper[:, :], hv, start=True, stop=True))
            m = pe.run(lambda e, k=k, hv=hv: e.matmul(psum[2 + k][:, 0:hv.shape[1]], ones[:, :], hv, start=True, stop=True))
        dve.wait(m)
        for k, (t0, t1) in enumerate(cuts):
            w = (t1 - t0) * NE
            dve.run(lambda e, k=k, t0=t0, t1=t1, w=w: e.tensor_copy(
                tot[:, t0:t1, :].rearrange("p t e -> p (t e)"), psum[2 + k][:, 0:w]))
            m = dve.run(lambda e, k=k, t0=t0, t1=t1, w=w: e.tensor_copy(
                lg[:, t0:t1, :].rearrange("p t e -> p (t e)"), psum[k][:, 0:w]))
        zero = route_buf(T)
        m = dve.run(lambda e: e.memset(zero[:, :], 0.0))
        dve.wait(m)
        for x_ in range(NE):
            m = dve.run(lambda e, x_=x_: e.tensor_tensor_scan(tmp[:, :, x_], tot[:, :, x_], zero[:, :], 0.0,
                                                              ALU.add, ALU.add))
        dve.wait(m)
        dve.chain(lambda e: e.tensor_tensor(lg, lg, tmp, ALU.add))
        dve.chain(lambda e: e.tensor_tensor(lg, lg, tot, ALU.subtract))
        dve.chain(lambda e: e.tensor_tensor(lg, lg, hot, ALU.mult))
        dve.chain(lambda e: e.tensor_reduce(lo[:, :], lg, AX.X, ALU.add))
        dve.chain(lambda e: e.tensor_tensor(hot, hot, per_expert(e_base[:, :]), ALU.mult))
        dve.chain(lambda e: e.tensor_reduce(hi[:, :], hot, AX.X, ALU.add))
        dve.chain(lambda e: e.tensor_single_scalar(zero[:, :], lo[:, :], float(CAP), ALU.is_le))
        dve.chain(lambda e: e.tensor_tensor(zero[:, :], zero[:, :], c1[:, :], ALU.mult))
        dve.chain(lambda e: e.tensor_scalar(zero[:, :], zero[:, :], -1024.0, 1024.0, ALU.mult, ALU.add))
        dve.chain(lambda e: e.tensor_tensor(hi[:, :], hi[:, :], zero[:, :], ALU.add))
        dve.chain(lambda e: e.tensor_single_scalar(lo[:, :], lo[:, :], 1.0, ALU.subtract))
        dve.chain(lambda e: e.tensor_copy(pos_i[:, :], lo[:, :]))
        dve.chain(lambda e: e.tensor_single_scalar(pos_i[:, :], pos_i[:, :], P - 1, ALU.bitwise_and))
        dve.chain(lambda e: e.tensor_copy(c1[:, :], pos_i[:, :]))
        dve.chain(lambda e: e.tensor_tensor(lo[:, :], lo[:, :], c1[:, :], ALU.subtract))
        dve.chain(lambda e: e.tensor_single_scalar(lo[:, :], lo[:, :], 1.0 / P, ALU.mult))
        routed = dve.chain(lambda e: e.tensor_tensor(hi[:, :], hi[:, :], lo[:, :], ALU.add))

        U_E = -(-SLOT_TILES // GE)
        before_e.close()

        def sb_e(name, shape):
            return ctx.enter_context(nc.sbuf_tensor(name, shape, F32, side="right"))
        w_raw = sb_e("w_raw", [P, EXPERT_W])
        w_parts = [[sb_e(f"w{i}_{part}", [P, EXPERT_W]) for part in ("hi", "lo")] for i in range(2)]
        hid = sb_e("hid", [P, 2, HID_W])
        xg_hl = sb_e("xg_hl", [P, 2, 2 * H * GE * P])
        RELU_SLOTS = 3
        relu = sb_e("relu", [P, RELU_SLOTS, GE * P])
        b2_slots = [w[:, h, :] for w in (weff, w2m_sb) for h in range(H)][0:3]
        w_ld = [slot(f"w_ld{i}") for i in range(2)]
        b1_ld = slot("b1_ld")
        weights_loaded, weights_ready, second_done, biased = {}, {}, {}, {}

        def w1_w2(w):
            return (w[:, 0:H * FF].rearrange("p (h f) -> p h f", h=H),
                    w[:, H * FF:EXPERT_W].rearrange("p (c d) -> p c d", c=FC))

        def load_expert(x_):
            if x_ >= 1:
                sp.wait(weights_ready[x_ - 1])
            if x_ >= 3:
                sp.wait(biased[U_E * (x_ - 2) - 1])
            w1, w2 = w1_w2(w_raw)
            sp.dma(lambda e: e.dma_start(w1, ffn_w1[x_].rearrange("(h p) f -> p h f", p=P)), w_ld[x_ % 2])
            sp.dma(lambda e: e.dma_start(w2, ffn_w2[x_].rearrange("(c p) d -> p c d", p=P)), w_ld[x_ % 2])
            weights_loaded[x_] = sp.dma(lambda e: e.dma_start(
                b2_slots[x_ % 3], ffn_b2[x_:x_ + 1, :].broadcast_to([P, D])), w_ld[x_ % 2])

        def split_expert(x_, k, n):
            share = slice(k * EXPERT_W // n, (k + 1) * EXPERT_W // n)
            raw, hi, lo = (w[:, share] for w in (w_raw, *w_parts[x_ % 2]))
            pool.wait(weights_loaded[x_])
            if x_ >= 2:
                pool.wait(second_done[U_E * (x_ - 1) - 1])
            pool.chain(lambda e: e.tensor_copy(hi.bitcast(F32R), raw))
            weights_ready[x_] = pool.run(lambda e: e.tensor_tensor(lo.bitcast(F32R), raw, hi, ALU.subtract))

        sp.wait(state["acc_free"])
        load_expert(0)
        split_expert(0, 0, 1)
        fb1 = sb("fb1", [P, NE, FC])
        b1_loaded = sp.dma(lambda e: e.dma_start(fb1[:, :, :], ffn_b1), b1_ld)
        load_expert(1)

        at_row = route_buf(RT, P)
        at_col = route_buf(RT, 2 * TABLE)
        table_mm = {}
        for t in range(T):
            s = t % RT
            pool.wait(routed)
            if t >= RT:
                pool.wait(table_mm[t - RT])
                dve.wait(table_mm[t - RT])
            if t % 4 == 0:
                a = pool.run(lambda e, t=t, s=s: e.tensor_scalar(
                    at_row[:, s, :], iota_p[:, :], c1[:, t:t + 1], None, ALU.is_equal))
            else:
                act.wait(routed)
                if t >= RT:
                    act.wait(table_mm[t - RT])
                act.chain(lambda e, t=t, s=s: e.activation(
                    at_row[:, s, :], iota_p[:, :], ACT.Abs, bias=c1[:, t:t + 1], scale=-1.0))
                a = act.run(lambda e, s=s: e.activation(
                    at_row[:, s, :], at_row[:, s, :], ACT.Relu, bias=ones[:, 0:1], scale=-1.0))
            dve.run(lambda e, t=t, s=s: e.tensor_scalar(
                at_col[:, s, 0:TABLE], iota_p[:, 0:TABLE], hi[:, t:t + 1], ids[:, t:t + 1], ALU.is_equal, ALU.mult))
            lane = pool if t % 4 == 1 else dve
            d = lane.run(lambda e, t=t, s=s: e.tensor_scalar(
                at_col[:, s, TABLE:2 * TABLE], iota_p[:, 0:TABLE], hi[:, t:t + 1], prb[:, t:t + 1], ALU.is_equal, ALU.mult))
            pe.wait(a, d, (dve.done, dve.count))
            table_mm[t] = pe.run(lambda e, t=t, s=s: e.matmul(
                psum[4][:, 0:2 * TABLE], at_row[:, s, :], at_col[:, s, :], start=t == 0, stop=t == T - 1))
        gat_i = sb("gat_i", [P, TABLE], I32)
        sca_i = sb("sca_i", [P, TABLE], I32)
        sprb = upper[:, 0:TABLE]
        idf = route_buf(TABLE)
        empty = route_buf(TABLE)
        dve.wait(table_mm[T - 1])
        table_ready = dve.run(lambda e: e.tensor_scalar(gat_i[:, :], psum[4][:, 0:TABLE], 1.0, 0.0,
                                                        ALU.subtract, ALU.max))
        dve.run(lambda e: e.tensor_copy(sprb[:, :], psum[4][:, TABLE:2 * TABLE]))
        dve.chain(lambda e: e.tensor_single_scalar(idf[:, :], psum[4][:, 0:TABLE], 1.0, ALU.subtract))
        dve.chain(lambda e: e.tensor_single_scalar(empty[:, :], idf[:, :], 0.0, ALU.is_lt))
        dve.chain(lambda e: e.scalar_tensor_tensor(empty[:, :], empty[:, :], float(2 * N), idf[:, :], ALU.mult, ALU.add))
        scatter_ready = dve.chain(lambda e: e.tensor_copy(sca_i[:, :], empty[:, :]))

        RX = 3 * GE
        xs_slots = [rows_sb[:, i, :] for i in range(RX)]
        assert RX <= ROW_SLOTS
        YS = 3
        yo = sb_e("yo", [P, YS, 2, D])
        mask_sb = sb_e("mask_sb", [P, 2, D])
        clip_sb = sb_e("clip_sb", [P, 2, D])

        nil = sb("nil", [P, 1])
        xs_ld = [slot(f"xs_ld{i}") for i in range(RX)]
        y_st = [slot(f"y_st{i}") for i in range(YS)]
        consts_e = dve.run(lambda e: e.memset(nil[:, :], 0.0))
        dve.wait(consts_e)
        xs_free, tre_read, xgt_read, xg_ready = {}, {}, {}, {}
        rest_made, hidden = {}, {}
        relu_read, y_read, y_stored = {}, {}, {}
        c_readers = (logit_mm[C_UNITS - 1], side_read[C_UNITS - 1], table_ready)
        assert U_E >= 2
        units = [(x_, j) for x_ in range(NE) for j in range(U_E)]
        tr_n, s1_n, y_n = [0], [0], [0]

        def three(out_, stationary, moving, start, stop):
            (s_hi, s_lo), (m_hi, m_lo) = stationary, moving
            for k, (a, b) in enumerate(((s_hi, m_lo), (s_hi, m_hi), (s_lo, m_hi))):
                m = pe.run(lambda e, a=a, b=b, k=k: e.matmul(
                    out_, a.bitcast(F32R), b.bitcast(F32R), start=start and k == 0, stop=stop and k == 2),
                    tell=stop and k == 2)
            return m

        def finish_pair(k, i0, pair, bank, q):
            x_, j = units[k]
            o, col0 = q % YS, x_ * SLOT_TILES + j * GE + i0
            cuts = [(P, 0, len(pair))] if pair[-1] == P else [(r, i, i + 1) for i, r in enumerate(pair)]
            product = psum[bank][:, :].rearrange("p (i d) -> p i d", d=D)

            def all_of(step):
                for cut in cuts:
                    m = step(*cut)
                dve.wait(m)
                return m

            def y_of(r, a, b):
                return yo[0:r, o, a:b, :]

            def mask_of(r, a, b):
                return mask_sb[0:r, a:b, :].bitcast(I32)

            y_read[q] = all_of(lambda r, a, b: dve.run(lambda e: e.tensor_tensor(
                y_of(r, a, b), product[0:r, a:b, :],
                b2_slots[x_ % 3][0:r, :].unsqueeze(1).broadcast_to([r, b - a, D]), ALU.add)))
            act.wait(y_read[q])
            for i, r in enumerate(pair):
                col = col0 + i
                scaled = act.run(lambda e, i=i, r=r, col=col, o=o: e.activation(
                    yo[0:r, o, i, :], yo[0:r, o, i, :], ACT.Copy, scale=sprb[0:r, col:col + 1]))
            yield
            dve.wait(scaled)
            all_of(lambda r, a, b: dve.run(lambda e: e.tensor_tensor(
                mask_of(r, a, b), y_of(r, a, b), y_of(r, a, b), ALU.not_equal)))
            yield
            all_of(lambda r, a, b: dve.run(lambda e: e.copy_predicated(
                y_of(r, a, b), mask_of(r, a, b), nil[0:r, :].unsqueeze(2).broadcast_to([r, b - a, D]))))
            yield
            all_of(lambda r, a, b: dve.run(lambda e: e.tensor_scalar(
                clip_sb[0:r, a:b, :], y_of(r, a, b), 10000.0, -10000.0, ALU.min, ALU.max)))
            all_of(lambda r, a, b: dve.run(lambda e: e.tensor_scalar(
                mask_of(r, a, b), y_of(r, a, b), 0.0, 0.0, ALU.mult, ALU.not_equal)))
            yield
            finished = all_of(lambda r, a, b: dve.run(lambda e: e.copy_predicated(
                y_of(r, a, b), mask_of(r, a, b), clip_sb[0:r, a:b, :])))
            pool.wait(finished)
            for i, r in enumerate(pair):
                col = col0 + i
                y_stored[q] = pool.dma(lambda e, o=o, i=i, r=r, col=col: e.indirect_dma_start(
                    out=out, out_offset=bass.IndirectOffsetOnAxis(ap=sca_i[0:r, col:col + 1], axis=0),
                    in_=yo[0:r, o, i, :], in_offset=None, bounds_check=N - 1, oob_is_err=False,
                    compute_op=ALU.add), y_st[o])

        def sizes_of(k):
            j = units[k][1]
            return [min(P, CAP - a * P) for a in range(j * GE, min(j * GE + GE, SLOT_TILES))]

        def xg_of(k):
            return xg_hl[:, k % 2, :].rearrange("p (k h n) -> p k h n", k=2, h=H)

        got = {}

        def gather_unit(k):
            x_, j = units[k]
            for i, r in enumerate(sizes_of(k)):
                s, col = (k * GE + i) % RX, x_ * SLOT_TILES + j * GE + i
                if k >= RX // GE:
                    pool.wait(xs_free[k - RX // GE])
                got[k, i] = pool.dma(lambda e, s=s, col=col, r=r: e.indirect_dma_start(
                    out=xs_slots[s][0:r, :], out_offset=None, in_=h2_d,
                    in_offset=bass.IndirectOffsetOnAxis(ap=gat_i[0:r, col:col + 1], axis=0)), xs_ld[s])

        def turn_unit(k):
            xg = xg_of(k)
            for i, r in enumerate(sizes_of(k)):
                s, bank = (k * GE + i) % RX, tr_n[0] % 2
                pe.wait(got[k, i])
                if tr_n[0] >= 2:
                    pe.wait(tre_read[tr_n[0] - 2])
                for h in range(H):
                    m = pe.run(lambda e, h=h, s=s, r=r, bank=bank: e.transpose(
                        psum[bank][:, h * P:h * P + r], xs_slots[s][0:r, h * P:(h + 1) * P], ident[0:r, 0:r]),
                        tell=h == H - 1)
                xs_free[k] = m
                act.wait(m)
                if k >= 2:
                    act.wait(xgt_read[k - 2])
                hi, lo = (xg[:, q, :, i * P:i * P + r] for q in range(2))
                turned = psum[bank][:, 0:H * P].rearrange("p (h n) -> p h n", h=H)[:, :, 0:r]
                a = act.run(lambda e, hi=hi, turned=turned: e.copy(hi.bitcast(F32R), turned))
                dve.wait(a)
                tre_read[tr_n[0]] = xg_ready[k] = dve.run(lambda e, hi=hi, lo=lo, turned=turned: e.tensor_tensor(
                    lo.bitcast(F32R), turned, hi, ALU.subtract))
                tr_n[0] += 1
                yield

        def first_layer(k):
            x_, n, xg = units[k][0], sum(sizes_of(k)), xg_of(k)
            pe.wait(xg_ready[k], weights_ready[x_])
            if k >= 1:
                act.wait(second_done[k - 1])
            act.wait(b1_loaded)
            (w1_hi, _), (w1_lo, _) = (w1_w2(w) for w in w_parts[x_ % 2])
            for f in range(FC):
                c, cols = s1_n[0], slice(f * P, (f + 1) * P)
                bank = 2 + c % 3
                if c >= 3:
                    pe.wait(relu_read[c - 3])
                for h in range(H):
                    m = three(psum[bank][:, 0:n], (w1_hi[:, h, cols], w1_lo[:, h, cols]),
                              (xg[:, 0, h, 0:n], xg[:, 1, h, 0:n]), h == 0, h == H - 1)
                act.wait(m)
                hi, lo = (hid[:, q, f * GE * P:f * GE * P + n] for q in range(2))
                full = relu[:, c % RELU_SLOTS, 0:n]
                if c >= RELU_SLOTS:
                    act.wait(rest_made[c - RELU_SLOTS])
                act.run(lambda e, f=f, bank=bank, hi=hi: e.activation(
                    hi.bitcast(F32R), psum[bank][:, 0:n], ACT.Relu, bias=fb1[:, x_, f:f + 1]))
                relu_read[c] = act.run(lambda e, f=f, bank=bank, full=full: e.activation(
                    full, psum[bank][:, 0:n], ACT.Relu, bias=fb1[:, x_, f:f + 1]))
                dve.wait(relu_read[c])
                rest_made[c] = hidden[k, f] = dve.run(lambda e, hi=hi, lo=lo, full=full: e.tensor_tensor(
                    lo.bitcast(F32R), full, hi, ALU.subtract))
                s1_n[0] += 1
                yield
            xgt_read[k] = m

        def second_layer(k):
            x_, sizes = units[k][0], sizes_of(k)
            dve.wait(weights_loaded[x_])
            (_, w2_hi), (_, w2_lo) = (w1_w2(w) for w in w_parts[x_ % 2])
            finish = iter(())
            for i0 in range(0, len(sizes), 2):
                pair = sizes[i0:i0 + 2]
                q = y_n[0]
                bank = 5 + q % 3
                if q >= 3:
                    pe.wait(y_read[q - 3])
                for i, r in enumerate(pair, i0):
                    for f in range(FC):
                        pe.wait(hidden[k, f])
                        at = slice(f * GE * P + i * P, f * GE * P + i * P + r)
                        m = three(psum[bank][0:r, (i - i0) * D:(i - i0 + 1) * D], (hid[:, 0, at], hid[:, 1, at]),
                                  (w2_hi[:, f, :], w2_lo[:, f, :]), f == 0, f == FC - 1)
                for _ in finish:
                    pass
                dve.wait(m)
                if q >= YS:
                    dve.wait(y_stored[q - YS])
                finish = finish_pair(k, i0, pair, bank, q)
                next(finish)
                y_n[0] += 1
            second_done[k], biased[k] = m, y_read[y_n[0] - 1]
            return finish

        pool.wait(*c_readers, *c_stored)
        K = len(units)
        for k in range(min(RX // GE, K)):
            gather_unit(k)
        pool.wait(scatter_ready)
        for _ in turn_unit(0):
            pass
        finish = iter(())
        for k in range(-1, K):
            if k >= 0:
                finish = second_layer(k)
            turning = turn_unit(k + 2) if k + 2 < K else iter(())
            for piece, _ in enumerate(first_layer(k + 1) if k + 1 < K else ()):
                if piece % 2 == 1:
                    next(turning, None)
                next(finish, None)
            for _ in turning:
                pass
            for _ in finish:
                pass
            if k >= 0 and k + RX // GE < K:
                gather_unit(k + RX // GE)
            if k + 1 < K:
                x_, j = units[k + 1]
                if x_ + 1 < NE and j < U_E - 1:
                    split_expert(x_ + 1, j, U_E - 1)
                    if j == U_E - 2 and x_ + 2 < NE:
                        load_expert(x_ + 2)
        for q in range(max(0, y_n[0] - YS), y_n[0]):
            pool.wait(y_stored[q])
        sp.wait(*c_stored)

        block = ctx.enter_context(nc.Block())
        block.sync(sp.play)
        block.gpsimd(pool.play)
        block.tensor(pe.play)
        block.vector(dve.play)
        block.scalar(act.play)


def kernel(**inputs):
    import numpy as np
    import concourse.bacc as bacc
    from concourse import mybir as my
    from concourse.bass_utils import run_bass_kernel_spmd

    given = {k: np.ascontiguousarray(v) for k, v in inputs.items()}
    n, d = given["x"].shape
    edges = given["src"].shape[0]
    unit = GROUP * P
    groups = -(-edges // unit)

    def padded(a, fill):
        whole = np.full(groups * unit, fill, a.dtype)
        whole[:edges] = a
        return whole

    def columns(a):
        return np.ascontiguousarray(a.reshape(groups * GROUP, P).T)

    per_row = next(k for k in range(-(-groups // P), groups + 1) if groups % k == 0)
    dst = padded(given["dst"], n)
    heads = d // HEADC
    w = given["L0_mix_w_qkv"].reshape(d, heads, 3, HEADC)
    b = given["L0_mix_b_qkv"].reshape(heads, 3, HEADC)

    def twice(name):
        return np.concatenate([np.tile(given[f"L0_mix_kln_{name}"], heads), np.tile(given[f"L0_mix_vln_{name}"], heads)])

    def by_partition(v):
        return np.ascontiguousarray(v.reshape(-1, P).T)

    b1 = given["L0_ffn_b1"]
    arrays = {
        "x": given["x"],
        "src": columns(padded(given["src"], 0)), "dst": columns(dst),
        "weight": columns(padded(given["edge_weight"], 0)),
        "dst_grouped": dst.reshape(groups // per_row, per_row * unit),
        "gnn_w1t": given["L0_gnn_W1"].T, "gnn_b1": given["L0_gnn_b1"],
        "gnn_w2t": given["L0_gnn_W2"].T, "gnn_b2": given["L0_gnn_b2"],
        "wqt_bq": np.concatenate([w[:, :, 0].reshape(d, d).T, b[:, 0].reshape(d, 1)], axis=1),
        "wkv": np.concatenate([w[:, :, 1].reshape(d, d), w[:, :, 2].reshape(d, d)], axis=1),
        "bkv": np.concatenate([b[:, 1].reshape(d), b[:, 2].reshape(d)]),
        "kv_gamma": twice("g"), "kv_beta": twice("b"),
        "mix_w1": given["L0_mix_w1"], "mix_b1": by_partition(given["L0_mix_b1"]),
        "mix_w2": given["L0_mix_w2"], "mix_b2": given["L0_mix_b2"],
        "gate_w": given["L0_ffn_gate_w"], "gate_b": given["L0_ffn_gate_b"],
        "ffn_w1": given["L0_ffn_w1"],
        "ffn_b1": b1.reshape(b1.shape[0], -1, P).transpose(2, 0, 1),
        "ffn_w2": given["L0_ffn_w2"], "ffn_b2": given["L0_ffn_b2"],
    }
    nc = bacc.Bacc("TRN2", target_bir_lowering=False, num_devices=1)
    feeds, args = {}, []
    for name, a in arrays.items():
        a = np.ascontiguousarray(a)
        feeds[f"{name}_in"] = a
        args.append(nc.dram_tensor(f"{name}_in", a.shape, my.dt.from_np(a.dtype), kind="ExternalInput").ap())
    args.append(nc.dram_tensor("out_dram", (n, d), my.dt.float32, kind="ExternalOutput").ap())
    build(nc, *args)
    ran = run_bass_kernel_spmd(nc, [feeds], core_ids=[0])
    return ran.results[0]["out_dram"]
```
